# Optimizing a Trainium2 kernel written in Bass

```python
import numpy as np
import jax
import jax.numpy as jnp

def _softmax(x, axis=-1):
    return jax.nn.softmax(x, axis=axis)

def _gelu(x):
    return jax.nn.gelu(x, approximate=True)

def _silu(x):
    return jax.nn.silu(x)

def _sigmoid(x):
    return jax.nn.sigmoid(x)

def _layernorm(x, axis=-1, eps=1e-05):
    m = jnp.mean(x, axis=axis, keepdims=True)
    v = jnp.var(x, axis=axis, keepdims=True)
    return (x - m) / jnp.sqrt(v + eps)

def _scatter_add(tgt, idx, src, axis=0):
    return tgt.at[idx].add(src)

def _segment_sum(src, seg, n):
    return jax.ops.segment_sum(src, seg, n)
kernel_name = 'mk_rec_standalone_d1_rec_r8_a96649'

def setup_inputs(seed: int=0):
    np.random.seed(seed)
    _w = jnp.asarray

    def _rec_inputs():
        import jax
        import jax.numpy as jnp
        _rk = jax.random.key(seed)
        r_dense_x = -0.00338568 + 1.0005 * jax.random.normal(jax.random.fold_in(_rk, 1), (2048, 13), jnp.float32)
        r_cat_idx = jnp.stack([jax.random.randint(jax.random.fold_in(jax.random.fold_in(_rk, 2), 0), (2048,), 2, 12500, jnp.int32), jax.random.randint(jax.random.fold_in(jax.random.fold_in(_rk, 2), 1), (2048,), 1, 99999, jnp.int32), jax.random.randint(jax.random.fold_in(jax.random.fold_in(_rk, 2), 2), (2048,), 0, 12500, jnp.int32), jax.random.randint(jax.random.fold_in(jax.random.fold_in(_rk, 2), 3), (2048,), 5, 12500, jnp.int32), jax.random.randint(jax.random.fold_in(jax.random.fold_in(_rk, 2), 4), (2048,), 20, 99993, jnp.int32), jax.random.randint(jax.random.fold_in(jax.random.fold_in(_rk, 2), 5), (2048,), 0, 99993, jnp.int32), jax.random.randint(jax.random.fold_in(jax.random.fold_in(_rk, 2), 6), (2048,), 2, 99999, jnp.int32), jax.random.randint(jax.random.fold_in(jax.random.fold_in(_rk, 2), 7), (2048,), 2, 99995, jnp.int32), jax.random.randint(jax.random.fold_in(jax.random.fold_in(_rk, 2), 8), (2048,), 0, 99999, jnp.int32), jax.random.randint(jax.random.fold_in(jax.random.fold_in(_rk, 2), 9), (2048,), 2, 99986, jnp.int32), jax.random.randint(jax.random.fold_in(jax.random.fold_in(_rk, 2), 10), (2048,), 4, 99999, jnp.int32), jax.random.randint(jax.random.fold_in(jax.random.fold_in(_rk, 2), 11), (2048,), 15, 99999, jnp.int32), jax.random.randint(jax.random.fold_in(jax.random.fold_in(_rk, 2), 12), (2048,), 0, 99989, jnp.int32), jax.random.randint(jax.random.fold_in(jax.random.fold_in(_rk, 2), 13), (2048,), 5, 99990, jnp.int32), jax.random.randint(jax.random.fold_in(jax.random.fold_in(_rk, 2), 14), (2048,), 2, 99996, jnp.int32), jax.random.randint(jax.random.fold_in(jax.random.fold_in(_rk, 2), 15), (2048,), 3, 99994, jnp.int32), jax.random.randint(jax.random.fold_in(jax.random.fold_in(_rk, 2), 16), (2048,), 0, 99998, jnp.int32), jax.random.randint(jax.random.fold_in(jax.random.fold_in(_rk, 2), 17), (2048,), 13, 99998, jnp.int32), jax.random.randint(jax.random.fold_in(jax.random.fold_in(_rk, 2), 18), (2048,), 10, 12498, jnp.int32), jax.random.randint(jax.random.fold_in(jax.random.fold_in(_rk, 2), 19), (2048,), 0, 99999, jnp.int32), jax.random.randint(jax.random.fold_in(jax.random.fold_in(_rk, 2), 20), (2048,), 0, 99995, jnp.int32), jax.random.randint(jax.random.fold_in(jax.random.fold_in(_rk, 2), 21), (2048,), 1, 99998, jnp.int32), jax.random.randint(jax.random.fold_in(jax.random.fold_in(_rk, 2), 22), (2048,), 1, 99997, jnp.int32), jax.random.randint(jax.random.fold_in(jax.random.fold_in(_rk, 2), 23), (2048,), 2, 99989, jnp.int32), jax.random.randint(jax.random.fold_in(jax.random.fold_in(_rk, 2), 24), (2048,), 6, 12500, jnp.int32), jax.random.randint(jax.random.fold_in(jax.random.fold_in(_rk, 2), 25), (2048,), 2, 99995, jnp.int32)], axis=1)
        return (r_dense_x, r_cat_idx)
    r_dense_x, r_cat_idx = _rec_inputs()

    def _L0_rec_setup():
        import jax, jax.numpy as jnp
        import numpy as np
        N_CAT, N_CONT, E, VOCAB = (26, 13, 128, 12500)
        B = 2048
        DENSE_DIMS = [512, 256]
        TOP_DIMS = [1024, 1024, 512, 256]
        N_PAIRS = (N_CAT + 1) * N_CAT // 2
        TOP_IN = N_PAIRS + E

        def _dense_params(key, dims):
            Ws, bs, ks = ([], [], jax.random.split(key, len(dims) - 1))
            for i, k in enumerate(ks):
                fan_in, fan_out = (dims[i], dims[i + 1])
                Ws.append(jax.random.normal(k, (fan_in, fan_out), jnp.float32) / np.sqrt(fan_in).astype(np.float32))
                bs.append(jnp.zeros((fan_out,), jnp.float32))
            return (Ws, bs)
        key = jax.random.key(seed)
        k_x, k_i, k_e, k_b, k_t = jax.random.split(key, 5)
        dense_x = jax.random.normal(k_x, (B, N_CONT), jnp.float32)
        cat_idx = jax.random.randint(k_i, (B, N_CAT), 0, VOCAB, jnp.int64)
        emb_table = jax.random.normal(k_e, (N_CAT, VOCAB, E), jnp.float32) * 0.01
        (Wd1, Wd2, Wdf), (bd1, bd2, bdf) = _dense_params(k_b, [N_CONT] + DENSE_DIMS + [E])
        (Wt1, Wt2, Wt3, Wt4, Wo), (bt1, bt2, bt3, bt4, bo) = _dense_params(k_t, [TOP_IN] + TOP_DIMS + [1])
        return dict(dense_x=dense_x, cat_idx=cat_idx, emb_table=emb_table, Wd1=Wd1, bd1=bd1, Wd2=Wd2, bd2=bd2, Wdf=Wdf, bdf=bdf, Wt1=Wt1, bt1=bt1, Wt2=Wt2, bt2=bt2, Wt3=Wt3, bt3=bt3, Wt4=Wt4, bt4=bt4, Wo=Wo, bo=bo)
    _L0_rec_all = _L0_rec_setup()
    _L0_rec_in = {k: v for k, v in _L0_rec_all.items() if k in ('emb_table', 'Wd1', 'bd1', 'Wd2', 'bd2', 'Wdf', 'bdf', 'Wt1', 'bt1', 'Wt2', 'bt2', 'Wt3', 'bt3', 'Wt4', 'bt4', 'Wo', 'bo')}
    del _L0_rec_all
    return {'r_dense_x': r_dense_x, 'r_cat_idx': r_cat_idx, 'L0_rec_emb_table': _L0_rec_in['emb_table'], 'L0_rec_Wd1': _L0_rec_in['Wd1'], 'L0_rec_bd1': _L0_rec_in['bd1'], 'L0_rec_Wd2': _L0_rec_in['Wd2'], 'L0_rec_bd2': _L0_rec_in['bd2'], 'L0_rec_Wdf': _L0_rec_in['Wdf'], 'L0_rec_bdf': _L0_rec_in['bdf'], 'L0_rec_Wt1': _L0_rec_in['Wt1'], 'L0_rec_bt1': _L0_rec_in['bt1'], 'L0_rec_Wt2': _L0_rec_in['Wt2'], 'L0_rec_bt2': _L0_rec_in['bt2'], 'L0_rec_Wt3': _L0_rec_in['Wt3'], 'L0_rec_bt3': _L0_rec_in['bt3'], 'L0_rec_Wt4': _L0_rec_in['Wt4'], 'L0_rec_bt4': _L0_rec_in['bt4'], 'L0_rec_Wo': _L0_rec_in['Wo'], 'L0_rec_bo': _L0_rec_in['bo']}

def reference(r_dense_x, r_cat_idx, L0_rec_emb_table, L0_rec_Wd1, L0_rec_bd1, L0_rec_Wd2, L0_rec_bd2, L0_rec_Wdf, L0_rec_bdf, L0_rec_Wt1, L0_rec_bt1, L0_rec_Wt2, L0_rec_bt2, L0_rec_Wt3, L0_rec_bt3, L0_rec_Wt4, L0_rec_bt4, L0_rec_Wo, L0_rec_bo):
    import jax
    import jax.numpy as jnp

    def _L0_rec_ref(dense_x, cat_idx, emb_table, Wd1, bd1, Wd2, bd2, Wdf, bdf, Wt1, bt1, Wt2, bt2, Wt3, bt3, Wt4, bt4, Wo, bo):
        import jax, jax.numpy as jnp
        import numpy as np
        N_CAT, N_CONT, E, VOCAB = (26, 13, 128, 12500)
        B = 2048
        DENSE_DIMS = [512, 256]
        TOP_DIMS = [1024, 1024, 512, 256]
        N_PAIRS = (N_CAT + 1) * N_CAT // 2
        TOP_IN = N_PAIRS + E

        def _dense_params(key, dims):
            Ws, bs, ks = ([], [], jax.random.split(key, len(dims) - 1))
            for i, k in enumerate(ks):
                fan_in, fan_out = (dims[i], dims[i + 1])
                Ws.append(jax.random.normal(k, (fan_in, fan_out), jnp.float32) / np.sqrt(fan_in).astype(np.float32))
                bs.append(jnp.zeros((fan_out,), jnp.float32))
            return (Ws, bs)
        fm = emb_table[jnp.arange(N_CAT)[None, :], cat_idx]
        h = jax.nn.relu(dense_x @ Wd1 + bd1)
        h = jax.nn.relu(h @ Wd2 + bd2)
        dense = jax.nn.relu(h @ Wdf + bdf)
        Z = jnp.concatenate([fm, dense[:, None, :]], axis=1)
        S = jnp.einsum('bie,bje->bij', Z, Z)
        iu, ju = np.triu_indices(N_CAT + 1, k=1)
        interactions = S[:, iu, ju]
        x = jnp.concatenate([interactions, dense], axis=-1)
        x = jax.nn.relu(x @ Wt1 + bt1)
        x = jax.nn.relu(x @ Wt2 + bt2)
        x = jax.nn.relu(x @ Wt3 + bt3)
        x = jax.nn.relu(x @ Wt4 + bt4)
        return jax.nn.sigmoid(x @ Wo + bo)
    y = _L0_rec_ref(r_dense_x, r_cat_idx, L0_rec_emb_table, L0_rec_Wd1, L0_rec_bd1, L0_rec_Wd2, L0_rec_bd2, L0_rec_Wdf, L0_rec_bdf, L0_rec_Wt1, L0_rec_bt1, L0_rec_Wt2, L0_rec_bt2, L0_rec_Wt3, L0_rec_bt3, L0_rec_Wt4, L0_rec_bt4, L0_rec_Wo, L0_rec_bo)
    return y

_drawn_inputs = setup_inputs


def setup_inputs(seed=0):
    import zlib

    import numpy as np

    out = dict(_drawn_inputs(seed))
    spreads = {'L0_rec_bd1': (0.0, 0.8),
     'L0_rec_bd2': (0.0, 0.8),
     'L0_rec_bdf': (0.0, 0.8),
     'L0_rec_bt1': (0.0, 2.0),
     'L0_rec_bt2': (0.0, 2.0),
     'L0_rec_bt3': (0.0, 2.0),
     'L0_rec_bt4': (0.0, 2.0)}
    factors = {'r_dense_x': 4.876,
     'L0_rec_emb_table': 8.0,
     'L0_rec_Wd1': 5.185,
     'L0_rec_Wd2': 5.556,
     'L0_rec_Wdf': 3.818,
     'L0_rec_Wt1': 4.328,
     'L0_rec_Wt2': 2.698,
     'L0_rec_Wt3': 4.112,
     'L0_rec_Wt4': 3.093,
     'L0_rec_Wo': 4.163}
    for name, (base, spread) in spreads.items():
        noise = np.random.default_rng([zlib.crc32(name.encode()), seed]).standard_normal(out[name].shape)
        drawn = base * np.exp(spread * noise) if base else spread * noise
        out[name] = jnp.asarray(drawn.astype(out[name].dtype))
    for name, factor in factors.items():
        out[name] = (out[name] * factor).astype(out[name].dtype)
    return out
```

```python
import numpy as np
import concourse.bass as bass
from concourse import mybir
from contextlib import ExitStack

F32 = mybir.dt.float32
F32R = mybir.dt.float32r
I32 = mybir.dt.int32
U32 = mybir.dt.uint32
ALU = mybir.AluOpType
ACT = mybir.ActivationFunctionType

P = 128
B, CONT, CATS, VOCAB, E = 2048, 13, 26, 12500, 128
FEATS = CATS + 1
PAIRS = FEATS * CATS // 2
CHUNK = 512
CHUNKS = B // CHUNK
TILES = CHUNK // P
S = 4
GROUPS = P // S
UNIT = 8
UNITS = GROUPS // UNIT
J = 32

FIRST_PAIR = [sum(FEATS - 1 - r for r in range(i)) for i in range(CATS)]
PAIR_BLOCKS = [(r, min(P, PAIRS - r)) for r in range(0, PAIRS, P)]
X_BLOCKS = PAIR_BLOCKS + [(PAIRS, E)]
FLIPS = [list(range(c, min(c + 4, CATS))) for c in range(0, CATS, 4)]
REGROUPS = [list(range(a, b)) for a, b in zip([0, 4, 8, 11, 14, 17, 20, 23], [4, 8, 11, 14, 17, 20, 23, 26])]

FULL = lambda n: [(k, P) for k in range(n)]
LAYERS = {
    "d2": ("h1", "h2", FULL(4), 2, 4),
    "df": ("h2", "dense", FULL(2), 1, 6),
    "t1": ("x", "h1", [(3, P)] + [(k, n) for k, (_, n) in enumerate(PAIR_BLOCKS)], 8, 7),
    "t2": ("h1", "h2", FULL(8), 8, 15),
    "t3": ("h2", "h1", FULL(8), 4, 23),
    "t4": ("h1", "h4", FULL(4), 2, 27),
}
BIASES = 29

BOTTOM = [s for half in range(2) for s in
          [("spread", half, m) for m in range(4)] + [("strip", half, "d2", m) for m in range(2)]
          + [("strip", half, "df", 0)]]
TOP = [("strip", 0, layer, m) for layer in ("t1", "t2", "t3", "t4") for m in range(LAYERS[layer][3])]
FEATURES = [s for k in range(TILES) for s in (("flip", k), ("pair", k))]
TAIL = [("dense", 0)] + [("stack", 0, b) for b in range(len(PAIR_BLOCKS))]


def mixed():
    before = {1: ("flip", 0), 2: ("pair", 0), 8: ("flip", 1), 9: ("pair", 1),
              12: ("flip", 2), 13: ("pair", 2), 16: ("flip", 3), 17: ("pair", 3), 20: ("regroup",)}
    out = []
    for n, s in enumerate(TOP):
        if n in before:
            out.append(before[n])
        out.append(s)
    return out + TAIL + [("out", 0)]


def counts(step):
    kind = step[0]
    split = kind in ("spread", "stack") or (kind == "strip" and step[2] not in ("df", "t4"))
    return {"acc": int(kind in ("spread", "strip", "stack", "out")), "split": int(split),
            "strip": int(kind == "strip"),
            "bank": len(FLIPS) if kind == "flip" else len(REGROUPS) if kind == "regroup" else 0,
            "unit": UNITS if kind == "pair" else 0, "tile": int(kind == "flip"), "dense": int(kind == "dense")}


KINDS = ("acc", "split", "strip", "bank", "unit", "tile", "dense")


def total(steps):
    return {k: sum(counts(s)[k] for s in steps) for k in KINDS}


def plus(*many):
    return {k: sum(m[k] for m in many) for k in KINDS}


class Place:

    def __init__(self, local, base, each, it):
        self.local, self.base, self.each, self.it = local, base, each, it

    def at(self, kind, more=0):
        return self.it * self.each[kind] + (self.base[kind] + self.local[kind] + more)

    def slot(self, kind, more=0):
        return (self.base[kind] + self.local[kind] + more) % 2


def walk(steps, base, it):
    local = {k: 0 for k in KINDS}
    each = total(steps)
    for step in steps:
        yield step, Place(dict(local), base, each, it)
        local = plus(local, counts(step))


PROLOGUE = FEATURES + [("regroup",)] + TAIL
BODY = mixed()
EPILOGUE = TOP + [("out", 0)]
ZERO = {k: 0 for k in KINDS}
AFTER_BOTTOM = plus(*[total(BOTTOM)] * (CHUNKS // 2))
AFTER_PROLOGUE = plus(AFTER_BOTTOM, total(PROLOGUE))
AFTER_BODY = plus(AFTER_PROLOGUE, *[total(BODY)] * (CHUNKS - 1))


def dlrm(nc, xT, idx, table, ident, w1, w, biases, wo, bo, out):
    ctx = ExitStack()
    with ctx:
        def sb(name, shape, dt=F32):
            return ctx.enter_context(nc.sbuf_tensor(name, shape, dt))

        def sem(name):
            return ctx.enter_context(nc.semaphore(name))

        gathered = sb("gathered", [P, 2, CATS, E])
        feats = sb("feats", [P, GROUPS, S, J])
        prods = sb("prods", [P, TILES * GROUPS, CATS])
        rows = sb("rows", [P, S, PAIRS])
        x = sb("x", [P, 2, len(X_BLOCKS), CHUNK], F32R)
        h1 = sb("h1", [P, 2, 8, CHUNK], F32R)
        h2 = sb("h2", [P, 2, 8, CHUNK], F32R)
        h4 = sb("h4", [P, 2, CHUNK])
        whole = sb("whole", [P, 2, CHUNK])
        dense = sb("dense", [P, B])
        raw = sb("raw", [P, 2, 8, P])
        strip = sb("strip", [P, 2, 2, 8, P], F32R)
        eye = sb("eye", [P, P])
        bias = sb("bias", [P, BIASES])
        wo_s = sb("wo_s", [P, 2])
        bo_s = sb("bo_s", [1, 1])
        cat = sb("cat", [P, CHUNKS * TILES, CATS], I32)
        first_row = sb("first_row", [P, CHUNKS * TILES, CATS], I32)
        row_of = sb("row_of", [P, CHUNKS * TILES, CATS], U32)
        tile_rows = sb("tile_rows", [P, 2, CATS], U32)
        y = sb("y", [1, B])

        bank = ctx.enter_context(nc.psum_tensor("bank", [P, 2, 512], F32))
        unit = ctx.enter_context(nc.psum_tensor("unit", [P, 2, UNIT, P], F32))
        acc = ctx.enter_context(nc.psum_tensor("acc", [P, 2, CHUNK], F32))

        inputs_in = sem("inputs_in")
        cat_in = sem("cat_in")
        raw_in = [sem("raw_in0"), sem("raw_in1")]
        gather_in = [sem("gather_in0"), sem("gather_in1")]
        y_out = sem("y_out")
        zeroed = sem("zeroed")
        first_row_set = sem("first_row_set")
        cat_step = sem("cat_step")
        rows_set = sem("rows_set")
        rows_seen = sem("rows_seen")
        wide_h = sem("wide_h")
        wide_ready = sem("wide_ready")
        low_w = sem("low_w")
        low_y = sem("low_y")
        low_dense = sem("low_dense")
        bank0_read = sem("bank0_read")
        unit_read_v = sem("unit_read_v")
        tile_flipped = sem("tile_flipped")
        high_w = sem("high_w")
        acc_read = sem("acc_read")
        high_dense = sem("high_dense")
        bank1_read = sem("bank1_read")
        unit_read_a = sem("unit_read_a")
        acc_done = sem("acc_done")
        bank_done = sem("bank_done")
        unit_done = sem("unit_done")

        regions = {"x": x, "h1": h1, "h2": h2}
        feats_flat = feats[:].rearrange("p g s j -> p (g s j)")
        wide_x_raw, wide_w_raw = feats_flat[:, 0:B], feats_flat[:, B:B + 512]
        wide_x = x[:, 0].rearrange("p k n -> p (k n)")
        wide_w = x[:, 1, 0, :]
        wrapped = prods[:, 0:CHUNKS * TILES, :]
        block = ctx.enter_context(nc.Block())

        def acc_target(step, p):
            if step[0] == "spread":
                return P, (h1[:, 0, step[2], :], h1[:, 1, step[2], :]), None, step[2]
            if step[0] == "stack":
                n = PAIR_BLOCKS[step[2]][1]
                return n, (x[0:n, 0, step[2], :], x[0:n, 1, step[2], :]), None, None
            _, dst, _, _, first = LAYERS[step[2]]
            m = step[3]
            if dst == "dense":
                return P, None, dense[:, bass.ts(p.it * 2 + step[1], CHUNK)], first
            if dst == "h4":
                return P, None, h4[:, m, :], first + m
            return P, (regions[dst][:, 0, m, :], regions[dst][:, 1, m, :]), None, first + m

        @block.sync
        def _(sp):
            sp.dma_start(cat[:], idx).then_inc(cat_in, 16)
            sp.wait_ge(zeroed, 1)
            for q in range(4):
                sp.dma_start(wide_x_raw[32 * q:32 * q + CONT], xT).then_inc(inputs_in, 16)
                sp.dma_start(wide_w_raw[32 * q:32 * q + CONT], w1).then_inc(inputs_in, 16)
            sp.dma_start(eye[:], ident).then_inc(inputs_in, 16)
            sp.dma_start(bias[:], biases).then_inc(inputs_in, 16)
            sp.dma_start(wo_s[:], wo).then_inc(inputs_in, 16)
            sp.dma_start(bo_s[:], bo).then_inc(inputs_in, 16)

            def load_strip(step, p):
                layer, m = step[2], step[3]
                slot = p.slot("strip")
                sp.wait_ge(low_w, p.at("strip", 1))
                cols = slice(m * P, (m + 1) * P)
                if layer == "t1":
                    a, c = PAIR_BLOCKS[2]
                    sp.dma_start(raw[:, slot, 0:2, :], w[layer][0:a, cols].rearrange("(k p) n -> p k n", p=P)
                                 ).then_inc(raw_in[slot], 16)
                    sp.dma_start(raw[0:c, slot, 2, :], w[layer][a:a + c, cols]).then_inc(raw_in[slot], 16)
                    sp.dma_start(raw[:, slot, 3, :], w[layer][PAIRS:PAIRS + E, cols]).then_inc(raw_in[slot], 16)
                else:
                    n = len(LAYERS[layer][2])
                    for k0, k1 in ((0, n // 2), (n // 2, n)):
                        sp.dma_start(raw[:, slot, k0:k1, :],
                                     w[layer][k0 * P:k1 * P, cols].rearrange("(k p) n -> p k n", p=P)
                                     ).then_inc(raw_in[slot], 16)
                    sp.sem_inc(raw_in[slot], 16)

            def phase(steps, base, it):
                for step, p in walk(steps, base, it):
                    if step[0] == "strip":
                        load_strip(step, p)

            with sp.Fori(0, CHUNKS // 2) as i:
                phase(BOTTOM, ZERO, i)
            with sp.Fori(0, CHUNKS - 1) as i:
                phase(BODY, AFTER_PROLOGUE, i)
            phase(EPILOGUE, AFTER_BODY, 0)
            sp.wait_ge(acc_read, 2 + AFTER_BODY["acc"] + total(EPILOGUE)["acc"])
            sp.dma_start(out.rearrange("b o -> o b"), y[:]).then_inc(y_out, 16)
            sp.wait_ge(y_out, 16)

        @block.gpsimd
        def _(pool):
            nc.gpsimd.iota(first_row[:], pattern=[[0, CHUNKS * TILES], [VOCAB, CATS]], base=0,
                           channel_multiplier=0).then_inc(first_row_set, 1)
            pool.wait_ge(cat_step, 4)

            def gather(t, k, copies):
                nc.gpsimd.tensor_copy(tile_rows[:, k, :], row_of[:, t, :]).then_inc(rows_set, 1)
                pool.wait_ge(rows_set, copies)
                pool.sem_inc(rows_seen, 1)
                for c in range(CATS):
                    nc.gpsimd.indirect_dma_start(
                        gathered[:, k, c, :], None, table,
                        bass.IndirectOffsetOnAxis(tile_rows[:, k, c:c + 1], 0)).then_inc(gather_in[k], 16)

            for k in range(2):
                gather(k, k, k + 1)
            with pool.Fori(1, CHUNKS * TILES // 2) as i:
                for k in range(2):
                    pool.wait_ge(tile_flipped, i * 2 + k - 1)
                    gather(i * 2 + k, k, i * 2 + k + 1)

        @block.vector
        def _(dve):
            nc.vector.memset(feats[:], 0.0).then_inc(zeroed, 1)
            dve.wait_ge(cat_in, 16)
            dve.wait_ge(first_row_set, 1)
            nc.vector.tensor_scalar(wrapped, cat[:], 0.0, float(VOCAB), ALU.is_lt, ALU.mult).then_inc(cat_step, 1)
            dve.wait_ge(cat_step, 1)
            nc.vector.tensor_tensor(wrapped, cat[:], wrapped, ALU.add).then_inc(cat_step, 1)
            dve.wait_ge(cat_step, 2)
            nc.vector.tensor_scalar(wrapped, wrapped, 0.0, float(VOCAB - 1), ALU.max, ALU.min).then_inc(cat_step, 1)
            dve.wait_ge(cat_step, 3)
            nc.vector.tensor_tensor(row_of[:], wrapped, first_row[:], ALU.add).then_inc(cat_step, 1)
            for k in range(2):
                nc.vector.memset(raw[:, k], 0.0).then_inc(low_w, 1)
            dve.sem_inc(low_y, 1)
            dve.wait_ge(inputs_in, 16 * 12)
            nc.vector.tensor_copy(wide_x, wide_x_raw).then_inc(wide_h, 1)
            nc.vector.tensor_copy(wide_w, wide_w_raw).then_inc(wide_h, 1)
            dve.wait_ge(wide_h, 2)
            for q in (32, 96):
                nc.vector.tensor_tensor(wide_x[q:q + 32], wide_x_raw[q:q + 32], wide_x[q:q + 32].bitcast(F32),
                                        ALU.subtract)
            nc.vector.tensor_tensor(wide_w[64:128], wide_w_raw[64:128], wide_w[64:128].bitcast(F32),
                                    ALU.subtract).then_inc(wide_ready, 1)

            def split_strip(p, more, blocks):
                slot = p.slot("strip", more)
                dve.wait_ge(high_w, p.at("strip", more + 1))
                nc.vector.tensor_tensor(strip[:, slot, 1, 0:blocks, :], raw[:, slot, 0:blocks, :],
                                        strip[:, slot, 0, 0:blocks, :].bitcast(F32), ALU.subtract
                                        ).then_inc(low_w, 1)

            def phase(steps, base, it, chunk, last=False):
                strips = [s for s in steps if s[0] == "strip"]
                for step, p in walk(steps, base, it):
                    kind = step[0]
                    if kind == "strip" and not (last and p.local["strip"] == len(strips) - 1):
                        after = p.local["strip"] + 1
                        split_strip(p, 1, len(LAYERS[strips[after][2]][2]) if after < len(strips) else 4)
                    if counts(step)["split"]:
                        n, parts, _, _ = acc_target(step, p)
                        dve.wait_ge(acc_read, p.at("acc", 3))
                        nc.vector.tensor_tensor(parts[1], whole[0:n, p.slot("acc"), :], parts[0].bitcast(F32),
                                                ALU.subtract).then_inc(low_y, 1)
                    if kind == "flip":
                        k = step[1]
                        for g, cats in enumerate(FLIPS):
                            if p.slot("bank", g) == 0:
                                dve.wait_ge(bank_done, p.at("bank", g + 1))
                                n = len(cats)
                                nc.vector.tensor_copy(
                                    feats[:, :, :, cats[0]:cats[0] + n].rearrange("p g s c -> p c s g"),
                                    bank[:, 0, 0:n * P].rearrange("p (c s g) -> p c s g", c=n, s=S)
                                ).then_inc(bank0_read, 1)
                        dve.wait_ge(bank_done, p.at("bank", len(FLIPS)))
                        nc.vector.tensor_copy(
                            feats[:, :, :, CATS].rearrange("p g s -> p s g"),
                            dense[:, bass.ts(chunk, CHUNK)].rearrange("p (s t g) -> p t s g", s=S, t=TILES)[:, k]
                        ).then_inc(tile_flipped, 1)
                    if kind == "pair":
                        k = step[1]
                        for u in range(UNITS):
                            dve.wait_ge(unit_done, p.at("unit", u + 1))
                            for s in range(0, S // 2):
                                last_read = nc.vector.tensor_copy(
                                    prods[J * s:J * s + J, k * GROUPS + u * UNIT:k * GROUPS + (u + 1) * UNIT, :],
                                    unit[J * s:J * s + J, p.slot("unit", u), :, CATS * s:CATS * (s + 1)])
                            last_read.then_inc(unit_read_v, 1)
                    if kind == "regroup":
                        for g, firsts in enumerate(REGROUPS):
                            if p.slot("bank", g) == 0:
                                dve.wait_ge(bank_done, p.at("bank", g + 1))
                                for q, i in enumerate(firsts):
                                    n = CATS - i
                                    last_read = nc.vector.tensor_copy(
                                        rows[:, :, FIRST_PAIR[i]:FIRST_PAIR[i] + n],
                                        bank[:, 0, q * P:(q + 1) * P].rearrange("p (s j) -> p s j", s=S)[:, :, i + 1:i + 1 + n])
                                last_read.then_inc(bank0_read, 1)
                    if kind == "dense":
                        dve.wait_ge(high_dense, p.at("dense", 1))
                        nc.vector.tensor_tensor(x[:, 1, 3, :], dense[:, bass.ts(chunk, CHUNK)],
                                                x[:, 0, 3, :].bitcast(F32), ALU.subtract).then_inc(low_dense, 1)

            split_strip(Place(ZERO, ZERO, ZERO, 0), 0, 4)
            with dve.Fori(0, CHUNKS // 2) as i:
                phase(BOTTOM, ZERO, i, None)
            dve.wait_ge(acc_read, 2 + AFTER_BOTTOM["acc"])
            phase(PROLOGUE, AFTER_BOTTOM, 0, 0)
            with dve.Fori(0, CHUNKS - 1) as i:
                phase(BODY, AFTER_PROLOGUE, i, i + 1)
            phase(EPILOGUE, AFTER_BODY, 0, None, last=True)

        @block.scalar
        def _(act):
            act.sem_inc(acc_read, 2)
            act.wait_ge(inputs_in, 16 * 12)

            def split_strip(p, more, blocks):
                slot = p.slot("strip", more)
                n = p.base["strip"] + p.local["strip"] + more
                act.wait_ge(raw_in[slot], p.it * (24 * p.each["strip"]) + 48 * (n // 2 + 1))
                nc.scalar.activation(strip[:, slot, 0, 0:blocks, :], raw[:, slot, 0:blocks, :],
                                     ACT.Copy).then_inc(high_w, 1)

            def splits_before(steps, p, n):
                return sum(counts(s)["split"] for s, q in walk(steps, ZERO, 0) if counts(s)["acc"] and q.local["acc"] <= n)

            def phase(steps, base, it, chunk, last=False):
                strips = [s for s in steps if s[0] == "strip"]
                for step, p in walk(steps, base, it):
                    kind = step[0]
                    if kind == "strip" and not (last and p.local["strip"] == len(strips) - 1):
                        after = p.local["strip"] + 1
                        split_strip(p, 1, len(LAYERS[strips[after][2]][2]) if after < len(strips) else 4)
                    if kind in ("spread", "strip", "stack"):
                        n, parts, plain, column = acc_target(step, p)
                        slot = p.slot("acc")
                        source = acc[0:n, slot, :]
                        func, b = (ACT.Copy, 0.0) if column is None else (ACT.Relu, bias[:, column:column + 1])
                        act.wait_ge(acc_done, p.at("acc", 1))
                        if parts is None:
                            nc.scalar.activation(plain, source, func, bias=b).then_inc(acc_read, 1)
                        else:
                            before = splits_before(steps, p, p.local["acc"] - 2)
                            act.wait_ge(low_y, p.it * p.each["split"] + (1 + p.base["split"] + before))
                            nc.scalar.activation(whole[0:n, slot, :], source, func, bias=b)
                            nc.scalar.activation(parts[0], source, func, bias=b).then_inc(acc_read, 1)
                    if kind == "out":
                        act.wait_ge(acc_done, p.at("acc", 1))
                        nc.scalar.activation(y[0:1, bass.ts(chunk - 1, CHUNK)], acc[0:1, p.slot("acc"), :],
                                             ACT.Sigmoid, bias=bo_s[0:1, 0:1]).then_inc(acc_read, 1)
                    if kind == "flip":
                        for g, cats in enumerate(FLIPS):
                            if p.slot("bank", g) == 1:
                                act.wait_ge(bank_done, p.at("bank", g + 1))
                                n = len(cats)
                                nc.scalar.activation(
                                    feats[:, :, :, cats[0]:cats[0] + n].rearrange("p g s c -> p c s g"),
                                    bank[:, 1, 0:n * P].rearrange("p (c s g) -> p c s g", c=n, s=S),
                                    ACT.Copy).then_inc(bank1_read, 1)
                    if kind == "pair":
                        k = step[1]
                        for u in range(UNITS):
                            act.wait_ge(unit_done, p.at("unit", u + 1))
                            for s in range(S // 2, S):
                                last_read = nc.scalar.activation(
                                    prods[J * s:J * s + J, k * GROUPS + u * UNIT:k * GROUPS + (u + 1) * UNIT, :],
                                    unit[J * s:J * s + J, p.slot("unit", u), :, CATS * s:CATS * (s + 1)], ACT.Copy)
                            last_read.then_inc(unit_read_a, 1)
                    if kind == "regroup":
                        for g, firsts in enumerate(REGROUPS):
                            if p.slot("bank", g) == 1:
                                act.wait_ge(bank_done, p.at("bank", g + 1))
                                for q, i in enumerate(firsts):
                                    n = CATS - i
                                    last_read = nc.scalar.activation(
                                        rows[:, :, FIRST_PAIR[i]:FIRST_PAIR[i] + n],
                                        bank[:, 1, q * P:(q + 1) * P].rearrange("p (s j) -> p s j", s=S)[:, :, i + 1:i + 1 + n],
                                        ACT.Copy)
                                last_read.then_inc(bank1_read, 1)
                    if kind == "dense":
                        nc.scalar.activation(x[:, 0, 3, :], dense[:, bass.ts(chunk, CHUNK)],
                                             ACT.Copy).then_inc(high_dense, 1)

            split_strip(Place(ZERO, ZERO, ZERO, 0), 0, 4)
            with act.Fori(0, CHUNKS // 2) as i:
                phase(BOTTOM, ZERO, i, None)
            act.wait_ge(acc_read, 2 + AFTER_BOTTOM["acc"])
            phase(PROLOGUE, AFTER_BOTTOM, 0, 0)
            with act.Fori(0, CHUNKS - 1) as i:
                phase(BODY, AFTER_PROLOGUE, i, i + 1)
            phase(EPILOGUE, AFTER_BODY, 0, CHUNKS, last=True)

        @block.tensor
        def _(pe):
            pe.wait_ge(wide_ready, 1)
            pe.wait_ge(inputs_in, 16 * 12)

            def phase(steps, base, it, chunk):
                for step, p in walk(steps, base, it):
                    kind = step[0]
                    slot = p.slot("acc")
                    if counts(step)["acc"]:
                        pe.wait_ge(acc_read, p.at("acc", 1))
                    if kind == "spread":
                        m = step[2]
                        nc.tensor.matmul(acc[:, slot, :], wide_w[:, m * P:(m + 1) * P],
                                         wide_x[:, bass.ts(p.it * 2 + step[1], CHUNK)],
                                         start=True, stop=True).then_inc(acc_done, 1)
                    if kind == "strip":
                        src, _, blocks, _, _ = LAYERS[step[2]]
                        m = step[3]
                        region = regions[src]
                        w_slot = p.slot("strip")
                        pe.wait_ge(low_w, p.at("strip", 3))
                        if m == 0 and src == "x":
                            pe.wait_ge(low_dense, p.at("dense"))
                        for n, (k, height) in enumerate(blocks):
                            if m == 0 and src != "x":
                                pe.wait_ge(low_y, p.at("split", 2 + k - len(blocks)))
                            if m == 0 and src == "x" and n == 1:
                                pe.wait_ge(low_y, p.at("split", 1))
                            for a, b in ((0, 0), (0, 1), (1, 0)):
                                last_mm = nc.tensor.matmul(
                                    acc[:, slot, :], strip[0:height, w_slot, a, k, :],
                                    region[0:height, b, k, :],
                                    start=(n == 0 and (a, b) == (0, 0)),
                                    stop=(n == len(blocks) - 1 and (a, b) == (1, 0)))
                        last_mm.then_inc(acc_done, 1)
                    if kind == "out":
                        pe.wait_ge(acc_read, p.at("acc", 2 - (len(PAIR_BLOCKS) if chunk is not None else 0)))
                        for k in range(2):
                            last_mm = nc.tensor.matmul(acc[0:1, slot, :], wo_s[:, k:k + 1], h4[:, k, :],
                                                       start=(k == 0), stop=(k == 1))
                        last_mm.then_inc(acc_done, 1)
                    if kind == "flip":
                        k = step[1]
                        t = p.local["tile"]
                        pe.wait_ge(gather_in[k % 2], p.it * (8 * CATS * TILES) + 16 * CATS * ((p.base["tile"] + t) // 2 + 1))
                        for g, cats in enumerate(FLIPS):
                            number = p.base["bank"] + p.local["bank"] + g
                            if number >= 2:
                                pe.wait_ge((bank0_read, bank1_read)[number % 2],
                                           p.it * (p.each["bank"] // 2) + number // 2)
                            for q, c in enumerate(cats):
                                last_t = nc.tensor.transpose(bank[:, number % 2, q * P:(q + 1) * P],
                                                             gathered[:, k % 2, c, :], eye[:])
                            last_t.then_inc(bank_done, 1)
                    if kind == "pair":
                        k = step[1]
                        banks = p.base["bank"] + p.local["bank"]
                        pe.wait_ge(tile_flipped, p.at("tile"))
                        pe.wait_ge(bank1_read, p.it * (p.each["bank"] // 2) + banks // 2)
                        for u in range(UNITS):
                            number = p.base["unit"] + p.local["unit"] + u
                            if number >= 2:
                                pe.wait_ge(unit_read_v, p.at("unit", u - 1))
                                pe.wait_ge(unit_read_a, p.at("unit", u - 1))
                            for v in range(UNIT):
                                group = feats[:, u * UNIT + v]
                                last_mm = nc.tensor.matmul(unit[:, number % 2, v, 0:S * CATS],
                                                           group.rearrange("p s j -> p (s j)"), group[:, :, 0:CATS],
                                                           start=True, stop=True)
                            last_mm.then_inc(unit_done, 1)
                    if kind == "regroup":
                        pe.wait_ge(unit_read_v, p.at("unit"))
                        pe.wait_ge(unit_read_a, p.at("unit"))
                        for g, firsts in enumerate(REGROUPS):
                            number = p.base["bank"] + p.local["bank"] + g
                            pe.wait_ge((bank0_read, bank1_read)[number % 2],
                                       p.it * (p.each["bank"] // 2) + number // 2)
                            for q, i in enumerate(firsts):
                                last_t = nc.tensor.transpose(bank[:, number % 2, q * P:(q + 1) * P],
                                                             prods[:, :, i], eye[:])
                            last_t.then_inc(bank_done, 1)
                    if kind == "stack":
                        first, n = PAIR_BLOCKS[step[2]]
                        if step[2] == 0:
                            banks = p.base["bank"] + p.local["bank"]
                            for s in (bank0_read, bank1_read):
                                pe.wait_ge(s, p.it * (p.each["bank"] // 2) + banks // 2)
                        for s in range(S):
                            last_t = nc.tensor.transpose(acc[0:n, slot, s * P:(s + 1) * P],
                                                         rows[:, s, first:first + n], eye[:])
                        last_t.then_inc(acc_done, 1)

            with pe.Fori(0, CHUNKS // 2) as i:
                phase(BOTTOM, ZERO, i, None)
            phase(PROLOGUE, AFTER_BOTTOM, 0, 0)
            with pe.Fori(0, CHUNKS - 1) as i:
                phase(BODY, AFTER_PROLOGUE, i, i)
            phase(EPILOGUE, AFTER_BODY, 0, None)


def kernel(r_dense_x, r_cat_idx, L0_rec_emb_table, L0_rec_Wd1, L0_rec_bd1, L0_rec_Wd2, L0_rec_bd2,
           L0_rec_Wdf, L0_rec_bdf, L0_rec_Wt1, L0_rec_bt1, L0_rec_Wt2, L0_rec_bt2, L0_rec_Wt3,
           L0_rec_bt3, L0_rec_Wt4, L0_rec_bt4, L0_rec_Wo, L0_rec_bo):
    import concourse.bacc as bacc
    from concourse.bass_utils import run_bass_kernel_spmd

    idx = np.asarray(r_cat_idx).reshape(CHUNKS, S, TILES, GROUPS, CATS).transpose(1, 3, 0, 2, 4)
    biases = np.concatenate([np.asarray(b).reshape(-1, P) for b in (
        L0_rec_bd1, L0_rec_bd2, L0_rec_bdf, L0_rec_bt1, L0_rec_bt2, L0_rec_bt3, L0_rec_bt4)])
    given = {
        "xT": np.asarray(r_dense_x).T,
        "idx": idx.reshape(P, CHUNKS * TILES, CATS),
        "table": np.asarray(L0_rec_emb_table).reshape(CATS * VOCAB, E),
        "ident": np.eye(P, dtype=np.float32),
        "w1": L0_rec_Wd1,
        "w_d2": L0_rec_Wd2, "w_df": L0_rec_Wdf,
        "w_t1": L0_rec_Wt1, "w_t2": L0_rec_Wt2, "w_t3": L0_rec_Wt3, "w_t4": L0_rec_Wt4,
        "biases": biases.T,
        "wo": np.asarray(L0_rec_Wo).reshape(2, P).T,
        "bo": np.asarray(L0_rec_bo).reshape(1, 1),
    }
    given = {k: np.ascontiguousarray(v) for k, v in given.items()}
    nc = bacc.Bacc("TRN2", target_bir_lowering=False, num_devices=1)
    ap = {k: nc.dram_tensor(k, v.shape, mybir.dt.from_np(v.dtype), kind="ExternalInput").ap()
          for k, v in given.items()}
    out = nc.dram_tensor("out", (B, 1), F32, kind="ExternalOutput").ap()
    dlrm(nc, ap["xT"], ap["idx"], ap["table"], ap["ident"], ap["w1"],
         {k: ap["w_" + k] for k in LAYERS}, ap["biases"], ap["wo"], ap["bo"], out)
    r = run_bass_kernel_spmd(nc, [given], core_ids=[0])
    return r.results[0]["out"]
```

```python
import numpy as np
import concourse.bass as bass
from concourse import mybir
from contextlib import ExitStack

F32 = mybir.dt.float32
F32R = mybir.dt.float32r
I32 = mybir.dt.int32
U32 = mybir.dt.uint32
ALU = mybir.AluOpType
ACT = mybir.ActivationFunctionType

P = 128
B, CONT, CATS, VOCAB, E = 2048, 13, 26, 12500, 128
FEATS = CATS + 1
PAIRS = FEATS * CATS // 2
CHUNK = 512
CHUNKS = B // CHUNK
TILES = CHUNK // P
S = 4
GROUPS = P // S
UNIT = 16
UNITS = GROUPS // UNIT
J = 32
BANKS = 4

FIRST_PAIR = [sum(FEATS - 1 - r for r in range(i)) for i in range(CATS)]
PAIR_BLOCKS = [(r, min(P, PAIRS - r)) for r in range(0, PAIRS, P)]
X_BLOCKS = PAIR_BLOCKS + [(PAIRS, E)]
FLIPS = [list(range(c, min(c + 4, CATS))) for c in range(0, CATS, 4)]
REGROUPS = [list(range(a, b)) for a, b in zip([0, 4, 8, 11, 14, 17, 20, 23], [4, 8, 11, 14, 17, 20, 23, 26])]

FULL = lambda n: [(k, P) for k in range(n)]
LAYERS = {
    "d2": ("h1", "h2", FULL(4), 2, 4),
    "df": ("h2", "dense", FULL(2), 1, 6),
    "t1": ("x", "h1", [(3, P)] + [(k, n) for k, (_, n) in enumerate(PAIR_BLOCKS)], 8, 7),
    "t2": ("h1", "h2", FULL(8), 8, 15),
    "t3": ("h2", "h1", FULL(8), 4, 23),
    "t4": ("h1", "h4", FULL(4), 2, 27),
}
BIASES = 29

BOTTOM = [s for half in range(2) for s in
          [("spread", half, m) for m in range(4)] + [("strip", half, "d2", m) for m in range(2)]
          + [("strip", half, "df", 0)]]
TOP = [("strip", 0, layer, m) for layer in ("t1", "t2", "t3", "t4") for m in range(LAYERS[layer][3])]
FEATURES = [s for k in range(TILES) for s in (("flip", k, 0), ("flip", k, 1), ("pair", k))]
HALVES = {"flip": (range(0, 4), range(4, len(FLIPS))), "regroup": (range(0, 4), range(4, len(REGROUPS)))}
FEATURES_AT = (6, 10, 14, 17)
REGROUP_AT = 20
STACK_AT = (22, 22, 22)


def mixed():
    before = {n: [] for n in range(len(TOP) + 1)}
    for k, n in enumerate(FEATURES_AT):
        for more, s in enumerate((("flip", k, 0), ("flip", k, 1), ("pair", k))):
            before[n + more].append(s)
    before[REGROUP_AT].append(("regroup", 0, 0))
    before[REGROUP_AT + 1] += [("regroup", 0, 1), ("dense", 0)]
    for b, n in enumerate(STACK_AT):
        before[n].append(("stack", 0, b))
    out = []
    for n, s in enumerate(TOP):
        out += before[n] + [s]
    return out + before[len(TOP)] + [("out", 0)]


def counts(step):
    kind = step[0]
    split = kind in ("spread", "stack") or (kind == "strip" and step[2] not in ("df", "t4"))
    return {"acc": int(kind in ("spread", "strip", "stack", "out")), "split": int(split),
            "strip": int(kind == "strip"),
            "bank": len(HALVES[kind][step[2]]) if kind in HALVES else 0,
            "unit": UNITS if kind == "pair" else 0, "tile": int(kind == "flip" and step[2] == 1),
            "dense": int(kind == "dense")}


KINDS = ("acc", "split", "strip", "bank", "unit", "tile", "dense")


def total(steps):
    return {k: sum(counts(s)[k] for s in steps) for k in KINDS}


def plus(*many):
    return {k: sum(m[k] for m in many) for k in KINDS}


class Place:

    def __init__(self, local, base, each, it):
        self.local, self.base, self.each, self.it = local, base, each, it

    def at(self, kind, more=0):
        return self.it * self.each[kind] + (self.base[kind] + self.local[kind] + more)

    def slot(self, kind, more=0):
        return (self.base[kind] + self.local[kind] + more) % 2


def walk(steps, base, it):
    local = {k: 0 for k in KINDS}
    each = total(steps)
    for step in steps:
        yield step, Place(dict(local), base, each, it)
        local = plus(local, counts(step))


BODY = mixed()
EPILOGUE = TOP + [("out", 0)]
FIRST = FEATURES[3:] + [("regroup", 0, 0), ("regroup", 0, 1), ("dense", 0)] + [
    ("stack", 0, b) for b in range(len(PAIR_BLOCKS))]
ZERO = {k: 0 for k in KINDS}
AFTER_HALF = total(BOTTOM)
AFTER_TILE = plus(AFTER_HALF, total(FEATURES[:3]))
AFTER_BOTTOM = plus(AFTER_TILE, total(BOTTOM))
AFTER_FIRST = plus(AFTER_BOTTOM, total(FIRST))
AFTER_BODY = plus(AFTER_FIRST, *[total(BODY)] * (CHUNKS - 1))


def dlrm(nc, xT, idx, table, ident, w1, w, biases, wo, bo, out):
    ctx = ExitStack()
    with ctx:
        def sb(name, shape, dt=F32):
            return ctx.enter_context(nc.sbuf_tensor(name, shape, dt))

        def sem(name):
            return ctx.enter_context(nc.semaphore(name))

        gathered = sb("gathered", [P, 2, CATS, E])
        feats = sb("feats", [P, GROUPS, S, FEATS])
        prods = sb("prods", [P, TILES * GROUPS, CATS])
        rows = sb("rows", [P, S, PAIRS])
        x = sb("x", [P, 2, len(X_BLOCKS), CHUNK], F32R)
        h1 = sb("h1", [P, 2, 8, CHUNK], F32R)
        h2 = sb("h2", [P, 2, 8, CHUNK], F32R)
        h4 = sb("h4", [P, 2, CHUNK])
        whole = sb("whole", [P, 2, CHUNK])
        dense = sb("dense", [P, B])
        raw = sb("raw", [P, 2, 8, P])
        strip = sb("strip", [P, 2, 2, 8, P], F32R)
        eye = sb("eye", [P, P])
        bias = sb("bias", [P, BIASES])
        wo_s = sb("wo_s", [P, 2])
        bo_s = sb("bo_s", [1, 1])
        cat = sb("cat", [P, CHUNKS * TILES, CATS], I32)
        first_row = sb("first_row", [P, CHUNKS * TILES, CATS], I32)
        row_of = sb("row_of", [P, CHUNKS * TILES, CATS], U32)
        tile_rows = sb("tile_rows", [P, 2, CATS], U32)
        y = sb("y", [1, B])

        bank = ctx.enter_context(nc.psum_tensor("bank", [P, BANKS, 512], F32))
        unit = ctx.enter_context(nc.psum_tensor("unit", [P, 2, 512], F32))
        acc = ctx.enter_context(nc.psum_tensor("acc", [P, 2, CHUNK], F32))

        inputs_in = sem("inputs_in")
        cat_in = sem("cat_in")
        raw_in = [sem("raw_in0"), sem("raw_in1")]
        gather_in = [sem("gather_in0"), sem("gather_in1")]
        y_out = sem("y_out")
        zeroed = sem("zeroed")
        first_row_set = sem("first_row_set")
        cat_step = sem("cat_step")
        rows_set = sem("rows_set")
        rows_seen = sem("rows_seen")
        unit_zeroed = sem("unit_zeroed")
        wide_h = sem("wide_h")
        wide_ready = sem("wide_ready")
        low_w = sem("low_w")
        low_y = sem("low_y")
        low_dense = sem("low_dense")
        even_bank_read = sem("even_bank_read")
        even_unit_read = sem("even_unit_read")
        tile_flipped = sem("tile_flipped")
        high_w = sem("high_w")
        acc_read = sem("acc_read")
        high_dense = sem("high_dense")
        odd_bank_read = sem("odd_bank_read")
        odd_unit_read = sem("odd_unit_read")
        acc_done = sem("acc_done")
        bank_done = sem("bank_done")
        unit_done = sem("unit_done")

        regions = {"x": x, "h1": h1, "h2": h2}
        feats_flat = feats[:].rearrange("p g s j -> p (g s j)")
        wide_x_raw, wide_w_raw = feats_flat[:, 0:B], feats_flat[:, B:B + 512]
        wide_x = x[:, 0].rearrange("p k n -> p (k n)")
        wide_w = x[:, 1, 0, :]
        products = [unit[:, u, 0:UNIT * CATS].rearrange("p (g i) -> p g i", i=CATS) for u in range(2)]
        wrapped = prods[:, 0:CHUNKS * TILES, :]
        block = ctx.enter_context(nc.Block())

        def chunk_of(step, p):
            return step[1] + 2 * (p.base["acc"] > 0)

        def acc_target(step, p):
            if step[0] == "spread":
                return P, (h1[:, 0, step[2], :], h1[:, 1, step[2], :]), None, step[2]
            if step[0] == "stack":
                n = PAIR_BLOCKS[step[2]][1]
                return n, (x[0:n, 0, step[2], :], x[0:n, 1, step[2], :]), None, None
            _, dst, _, _, first = LAYERS[step[2]]
            m = step[3]
            if dst == "dense":
                return P, None, dense[:, bass.ts(chunk_of(step, p), CHUNK)], first
            if dst == "h4":
                return P, None, h4[:, m, :], first + m
            return P, (regions[dst][:, 0, m, :], regions[dst][:, 1, m, :]), None, first + m

        def bank_copies(kind, n, slot):
            if kind == "flip":
                c, m = FLIPS[n][0], len(FLIPS[n])
                return [(feats[:, :, :, c:c + m].rearrange("p g s c -> p c s g"),
                         bank[:, slot, 0:m * P].rearrange("p (c s g) -> p c s g", c=m, s=S))]
            return [(rows[:, :, FIRST_PAIR[i]:FIRST_PAIR[i] + CATS - i],
                     bank[:, slot, q * P:(q + 1) * P].rearrange("p (s j) -> p s j", s=S)[:, :, i + 1:FEATS])
                    for q, i in enumerate(REGROUPS[n])]

        def unit_target(k, u):
            return prods[:, k * GROUPS + u * UNIT:k * GROUPS + (u + 1) * UNIT, :]

        @block.sync
        def _(sp):
            sp.dma_start(cat[:], idx).then_inc(cat_in, 16)
            sp.wait_ge(zeroed, 1)
            for q in range(4):
                sp.dma_start(wide_x_raw[32 * q:32 * q + CONT], xT).then_inc(inputs_in, 16)
                sp.dma_start(wide_w_raw[32 * q:32 * q + CONT], w1).then_inc(inputs_in, 16)
            sp.dma_start(eye[:], ident).then_inc(inputs_in, 16)
            sp.dma_start(bias[:], biases).then_inc(inputs_in, 16)
            sp.dma_start(wo_s[:], wo).then_inc(inputs_in, 16)
            sp.dma_start(bo_s[:], bo).then_inc(inputs_in, 16)

            def load_strip(step, p):
                layer, m = step[2], step[3]
                slot = p.slot("strip")
                sp.wait_ge(low_w, p.at("strip", 1))
                cols = slice(m * P, (m + 1) * P)
                if layer == "t1":
                    a, c = PAIR_BLOCKS[2]
                    sp.dma_start(raw[:, slot, 0:2, :], w[layer][0:a, cols].rearrange("(k p) n -> p k n", p=P)
                                 ).then_inc(raw_in[slot], 16)
                    sp.dma_start(raw[0:c, slot, 2, :], w[layer][a:a + c, cols]).then_inc(raw_in[slot], 16)
                    sp.dma_start(raw[:, slot, 3, :], w[layer][PAIRS:PAIRS + E, cols]).then_inc(raw_in[slot], 16)
                else:
                    n = len(LAYERS[layer][2])
                    for k0, k1 in ((0, n // 2), (n // 2, n)):
                        sp.dma_start(raw[:, slot, k0:k1, :],
                                     w[layer][k0 * P:k1 * P, cols].rearrange("(k p) n -> p k n", p=P)
                                     ).then_inc(raw_in[slot], 16)
                    sp.sem_inc(raw_in[slot], 16)

            def phase(steps, base, it):
                for step, p in walk(steps, base, it):
                    if step[0] == "strip":
                        load_strip(step, p)

            phase(BOTTOM, ZERO, 0)
            phase(BOTTOM, AFTER_TILE, 0)
            with sp.Fori(0, CHUNKS - 1) as i:
                phase(BODY, AFTER_FIRST, i)
            phase(EPILOGUE, AFTER_BODY, 0)
            sp.wait_ge(acc_read, 2 + AFTER_BODY["acc"] + total(EPILOGUE)["acc"])
            sp.dma_start(out.rearrange("b o -> o b"), y[:]).then_inc(y_out, 16)
            sp.wait_ge(y_out, 16)

        @block.gpsimd
        def _(pool):
            nc.gpsimd.iota(first_row[:], pattern=[[0, CHUNKS * TILES], [VOCAB, CATS]], base=0,
                           channel_multiplier=0).then_inc(first_row_set, 1)
            pool.wait_ge(cat_step, 4)

            def gather(t, k, copies):
                nc.gpsimd.tensor_copy(tile_rows[:, k, :], row_of[:, t, :]).then_inc(rows_set, 1)
                pool.wait_ge(rows_set, copies)
                pool.sem_inc(rows_seen, 1)
                for c in range(CATS):
                    nc.gpsimd.indirect_dma_start(
                        gathered[:, k, c, :], None, table,
                        bass.IndirectOffsetOnAxis(tile_rows[:, k, c:c + 1], 0)).then_inc(gather_in[k], 16)

            for k in range(2):
                gather(k, k, k + 1)
            with pool.Fori(1, CHUNKS * TILES // 2) as i:
                for k in range(2):
                    pool.wait_ge(tile_flipped, i * 2 + k - 1)
                    gather(i * 2 + k, k, i * 2 + k + 1)

        @block.vector
        def _(dve):
            nc.vector.memset(feats[:], 0.0).then_inc(zeroed, 1)
            dve.wait_ge(cat_in, 16)
            dve.wait_ge(first_row_set, 1)
            nc.vector.tensor_scalar(wrapped, cat[:], 0.0, float(VOCAB), ALU.is_lt, ALU.mult).then_inc(cat_step, 1)
            dve.wait_ge(cat_step, 1)
            nc.vector.tensor_tensor(wrapped, cat[:], wrapped, ALU.add).then_inc(cat_step, 1)
            dve.wait_ge(cat_step, 2)
            nc.vector.tensor_scalar(wrapped, wrapped, 0.0, float(VOCAB - 1), ALU.max, ALU.min).then_inc(cat_step, 1)
            dve.wait_ge(cat_step, 3)
            nc.vector.tensor_tensor(row_of[:], wrapped, first_row[:], ALU.add).then_inc(cat_step, 1)
            for k in range(2):
                nc.vector.memset(raw[:, k], 0.0).then_inc(low_w, 1)
            dve.sem_inc(low_y, 1)
            nc.vector.memset(unit[:], 0.0).then_inc(unit_zeroed, 1)
            dve.wait_ge(inputs_in, 16 * 12)
            nc.vector.tensor_copy(wide_x, wide_x_raw).then_inc(wide_h, 1)
            nc.vector.tensor_copy(wide_w, wide_w_raw).then_inc(wide_h, 1)
            dve.wait_ge(wide_h, 2)
            for q in (32, 96):
                nc.vector.tensor_tensor(wide_x[q:q + 32], wide_x_raw[q:q + 32], wide_x[q:q + 32].bitcast(F32),
                                        ALU.subtract)
            nc.vector.tensor_tensor(wide_w[64:128], wide_w_raw[64:128], wide_w[64:128].bitcast(F32),
                                    ALU.subtract).then_inc(wide_ready, 1)

            def split_strip(p, more, blocks):
                slot = p.slot("strip", more)
                dve.wait_ge(high_w, p.at("strip", more + 1))
                nc.vector.tensor_tensor(strip[:, slot, 1, 0:blocks, :], raw[:, slot, 0:blocks, :],
                                        strip[:, slot, 0, 0:blocks, :].bitcast(F32), ALU.subtract
                                        ).then_inc(low_w, 1)

            def phase(steps, base, it, chunk, last=False):
                strips = [s for s in steps if s[0] == "strip"]
                for step, p in walk(steps, base, it):
                    kind = step[0]
                    if kind == "strip" and not (last and p.local["strip"] == len(strips) - 1):
                        after = p.local["strip"] + 1
                        split_strip(p, 1, len(LAYERS[strips[after][2]][2]) if after < len(strips) else 4)
                    if counts(step)["split"]:
                        n, parts, _, _ = acc_target(step, p)
                        dve.wait_ge(acc_read, p.at("acc", 3))
                        nc.vector.tensor_tensor(parts[1], whole[0:n, p.slot("acc"), :], parts[0].bitcast(F32),
                                                ALU.subtract).then_inc(low_y, 1)
                    if kind in HALVES:
                        for g, n in enumerate(HALVES[kind][step[2]]):
                            number = p.base["bank"] + p.local["bank"] + g
                            if number % 2 == 0:
                                dve.wait_ge(bank_done, p.at("bank", g + 1))
                                for to, source in bank_copies(kind, n, number % BANKS):
                                    last_read = nc.vector.tensor_copy(to, source)
                                last_read.then_inc(even_bank_read, 1)
                    if kind == "flip" and step[2] == 1:
                        dve.wait_ge(bank_done, p.at("bank", counts(step)["bank"]))
                        nc.vector.tensor_copy(
                            feats[:, :, :, CATS].rearrange("p g s -> p s g"),
                            dense[:, bass.ts(chunk, CHUNK)].rearrange("p (s t g) -> p t s g", s=S, t=TILES)[:, step[1]]
                        ).then_inc(tile_flipped, 1)
                    if kind == "pair":
                        for u in range(0, UNITS, 2):
                            dve.wait_ge(unit_done, p.at("unit", u + 1))
                            nc.vector.tensor_copy(unit_target(step[1], u), products[0]).then_inc(even_unit_read, 1)
                    if kind == "dense":
                        dve.wait_ge(high_dense, p.at("dense", 1))
                        nc.vector.tensor_tensor(x[:, 1, 3, :], dense[:, bass.ts(chunk, CHUNK)],
                                                x[:, 0, 3, :].bitcast(F32), ALU.subtract).then_inc(low_dense, 1)

            split_strip(Place(ZERO, ZERO, ZERO, 0), 0, 4)
            phase(BOTTOM, ZERO, 0, 0)
            dve.wait_ge(acc_read, 2 + AFTER_HALF["acc"])
            phase(FEATURES[:3], AFTER_HALF, 0, 0)
            phase(BOTTOM, AFTER_TILE, 0, 0)
            dve.wait_ge(acc_read, 2 + AFTER_BOTTOM["acc"])
            phase(FIRST, AFTER_BOTTOM, 0, 0)
            with dve.Fori(0, CHUNKS - 1) as i:
                phase(BODY, AFTER_FIRST, i, i + 1)
            phase(EPILOGUE, AFTER_BODY, 0, None, last=True)

        @block.scalar
        def _(act):
            act.sem_inc(acc_read, 2)
            act.wait_ge(inputs_in, 16 * 12)

            def split_strip(p, more, blocks):
                slot = p.slot("strip", more)
                n = p.base["strip"] + p.local["strip"] + more
                act.wait_ge(raw_in[slot], p.it * (24 * p.each["strip"]) + 48 * (n // 2 + 1))
                nc.scalar.activation(strip[:, slot, 0, 0:blocks, :], raw[:, slot, 0:blocks, :],
                                     ACT.Copy).then_inc(high_w, 1)

            def splits_before(steps, p, n):
                return sum(counts(s)["split"] for s, q in walk(steps, ZERO, 0) if counts(s)["acc"] and q.local["acc"] <= n)

            def phase(steps, base, it, chunk, last=False):
                strips = [s for s in steps if s[0] == "strip"]
                for step, p in walk(steps, base, it):
                    kind = step[0]
                    if kind == "strip" and not (last and p.local["strip"] == len(strips) - 1):
                        after = p.local["strip"] + 1
                        split_strip(p, 1, len(LAYERS[strips[after][2]][2]) if after < len(strips) else 4)
                    if kind in ("spread", "strip", "stack"):
                        n, parts, plain, column = acc_target(step, p)
                        slot = p.slot("acc")
                        source = acc[0:n, slot, :]
                        func, b = (ACT.Copy, 0.0) if column is None else (ACT.Relu, bias[:, column:column + 1])
                        act.wait_ge(acc_done, p.at("acc", 1))
                        if parts is None:
                            nc.scalar.activation(plain, source, func, bias=b).then_inc(acc_read, 1)
                        else:
                            before = splits_before(steps, p, p.local["acc"] - 2)
                            act.wait_ge(low_y, p.it * p.each["split"] + (1 + p.base["split"] + before))
                            nc.scalar.activation(whole[0:n, slot, :], source, func, bias=b)
                            nc.scalar.activation(parts[0], source, func, bias=b).then_inc(acc_read, 1)
                    if kind == "out":
                        act.wait_ge(acc_done, p.at("acc", 1))
                        nc.scalar.activation(y[0:1, bass.ts(chunk - 1, CHUNK)], acc[0:1, p.slot("acc"), :],
                                             ACT.Sigmoid, bias=bo_s[0:1, 0:1]).then_inc(acc_read, 1)
                    if kind in HALVES:
                        for g, n in enumerate(HALVES[kind][step[2]]):
                            number = p.base["bank"] + p.local["bank"] + g
                            if number % 2 == 1:
                                act.wait_ge(bank_done, p.at("bank", g + 1))
                                for to, source in bank_copies(kind, n, number % BANKS):
                                    last_read = nc.scalar.activation(to, source, ACT.Copy)
                                last_read.then_inc(odd_bank_read, 1)
                    if kind == "pair":
                        for u in range(1, UNITS, 2):
                            act.wait_ge(unit_done, p.at("unit", u + 1))
                            nc.scalar.activation(unit_target(step[1], u), products[1], ACT.Copy
                                                 ).then_inc(odd_unit_read, 1)
                    if kind == "dense":
                        nc.scalar.activation(x[:, 0, 3, :], dense[:, bass.ts(chunk, CHUNK)],
                                             ACT.Copy).then_inc(high_dense, 1)

            split_strip(Place(ZERO, ZERO, ZERO, 0), 0, 4)
            phase(BOTTOM, ZERO, 0, 0)
            phase(FEATURES[:3], AFTER_HALF, 0, 0)
            phase(BOTTOM, AFTER_TILE, 0, 0)
            act.wait_ge(acc_read, 2 + AFTER_BOTTOM["acc"])
            phase(FIRST, AFTER_BOTTOM, 0, 0)
            with act.Fori(0, CHUNKS - 1) as i:
                phase(BODY, AFTER_FIRST, i, i + 1)
            phase(EPILOGUE, AFTER_BODY, 0, CHUNKS, last=True)

        @block.tensor
        def _(pe):
            pe.wait_ge(wide_ready, 1)
            pe.wait_ge(unit_zeroed, 1)
            pe.wait_ge(inputs_in, 16 * 12)

            def half_at(p, kind, more, up=False):
                return p.it * (p.each[kind] // 2) + (p.base[kind] + p.local[kind] + more + up) // 2

            def phase(steps, base, it):
                after_h4 = 0
                for step, p in walk(steps, base, it):
                    kind = step[0]
                    after_h4 = 0 if kind == "strip" else after_h4 + counts(step)["acc"]
                    slot = p.slot("acc")
                    if counts(step)["acc"]:
                        pe.wait_ge(acc_read, p.at("acc", 1))
                    if kind == "spread":
                        m = step[2]
                        nc.tensor.matmul(acc[:, slot, :], wide_w[:, m * P:(m + 1) * P],
                                         wide_x[:, bass.ts(chunk_of(step, p), CHUNK)],
                                         start=True, stop=True).then_inc(acc_done, 1)
                    if kind == "strip":
                        src, _, blocks, _, _ = LAYERS[step[2]]
                        m = step[3]
                        region = regions[src]
                        w_slot = p.slot("strip")
                        pe.wait_ge(low_w, p.at("strip", 3))
                        if m == 0 and src == "x":
                            pe.wait_ge(low_dense, p.at("dense"))
                        for n, (k, height) in enumerate(blocks):
                            if m == 0 and src != "x":
                                pe.wait_ge(low_y, p.at("split", 2 + k - len(blocks)))
                            if m == 0 and src == "x" and n == 1:
                                pe.wait_ge(low_y, p.at("split", 1))
                            for a, b in ((0, 0), (0, 1), (1, 0)):
                                last_mm = nc.tensor.matmul(
                                    acc[:, slot, :], strip[0:height, w_slot, a, k, :],
                                    region[0:height, b, k, :],
                                    start=(n == 0 and (a, b) == (0, 0)),
                                    stop=(n == len(blocks) - 1 and (a, b) == (1, 0)))
                        last_mm.then_inc(acc_done, 1)
                    if kind == "out":
                        pe.wait_ge(acc_read, p.at("acc", 2 - (after_h4 - 1)))
                        for k in range(2):
                            last_mm = nc.tensor.matmul(acc[0:1, slot, :], wo_s[:, k:k + 1], h4[:, k, :],
                                                       start=(k == 0), stop=(k == 1))
                        last_mm.then_inc(acc_done, 1)
                    if kind in HALVES:
                        if kind == "flip":
                            number = p.base["tile"] + p.local["tile"]
                            pe.wait_ge(gather_in[number % 2], p.it * (8 * CATS * TILES) + 16 * CATS * (number // 2 + 1))
                        else:
                            pe.wait_ge(even_unit_read, half_at(p, "unit", 0))
                            pe.wait_ge(odd_unit_read, half_at(p, "unit", 0))
                        for g, n in enumerate(HALVES[kind][step[2]]):
                            number = p.base["bank"] + p.local["bank"] + g
                            if number >= BANKS:
                                pe.wait_ge((even_bank_read, odd_bank_read)[number % 2], half_at(p, "bank", g - 2))
                            for q, one in enumerate((FLIPS, REGROUPS)[kind == "regroup"][n]):
                                source = gathered[:, step[1] % 2, one, :] if kind == "flip" else prods[:, :, one]
                                last_t = nc.tensor.transpose(bank[:, number % BANKS, q * P:(q + 1) * P],
                                                             source, eye[:])
                            last_t.then_inc(bank_done, 1)
                    if kind == "pair":
                        pe.wait_ge(tile_flipped, p.at("tile"))
                        pe.wait_ge(odd_bank_read, half_at(p, "bank", 0))
                        for u in range(UNITS):
                            number = p.base["unit"] + p.local["unit"] + u
                            if number >= 2:
                                pe.wait_ge((even_unit_read, odd_unit_read)[number % 2], half_at(p, "unit", u))
                            for v in range(UNIT):
                                for s in range(S):
                                    one = feats[:, u * UNIT + v, s, :]
                                    last_mm = nc.tensor.matmul(
                                        unit[J * s:J * s + FEATS, number % 2, v * CATS:(v + 1) * CATS],
                                        one, one[:, 0:CATS], start=True, stop=True)
                            last_mm.then_inc(unit_done, 1)
                    if kind == "stack":
                        first, n = PAIR_BLOCKS[step[2]]
                        if step[2] == 0:
                            for read in (even_bank_read, odd_bank_read):
                                pe.wait_ge(read, half_at(p, "bank", 0, up=read is even_bank_read))
                        for s in range(S):
                            last_t = nc.tensor.transpose(acc[0:n, slot, s * P:(s + 1) * P],
                                                         rows[:, s, first:first + n], eye[:])
                        last_t.then_inc(acc_done, 1)

            phase(BOTTOM, ZERO, 0)
            phase(FEATURES[:3], AFTER_HALF, 0)
            phase(BOTTOM, AFTER_TILE, 0)
            phase(FIRST, AFTER_BOTTOM, 0)
            with pe.Fori(0, CHUNKS - 1) as i:
                phase(BODY, AFTER_FIRST, i)
            phase(EPILOGUE, AFTER_BODY, 0)


def kernel(r_dense_x, r_cat_idx, L0_rec_emb_table, L0_rec_Wd1, L0_rec_bd1, L0_rec_Wd2, L0_rec_bd2,
           L0_rec_Wdf, L0_rec_bdf, L0_rec_Wt1, L0_rec_bt1, L0_rec_Wt2, L0_rec_bt2, L0_rec_Wt3,
           L0_rec_bt3, L0_rec_Wt4, L0_rec_bt4, L0_rec_Wo, L0_rec_bo):
    import concourse.bacc as bacc
    from concourse.bass_utils import run_bass_kernel_spmd

    idx = np.asarray(r_cat_idx).reshape(CHUNKS, S, TILES, GROUPS, CATS).transpose(1, 3, 0, 2, 4)
    biases = np.concatenate([np.asarray(b).reshape(-1, P) for b in (
        L0_rec_bd1, L0_rec_bd2, L0_rec_bdf, L0_rec_bt1, L0_rec_bt2, L0_rec_bt3, L0_rec_bt4)])
    given = {
        "xT": np.asarray(r_dense_x).T,
        "idx": idx.reshape(P, CHUNKS * TILES, CATS),
        "table": np.asarray(L0_rec_emb_table).reshape(CATS * VOCAB, E),
        "ident": np.eye(P, dtype=np.float32),
        "w1": L0_rec_Wd1,
        "w_d2": L0_rec_Wd2, "w_df": L0_rec_Wdf,
        "w_t1": L0_rec_Wt1, "w_t2": L0_rec_Wt2, "w_t3": L0_rec_Wt3, "w_t4": L0_rec_Wt4,
        "biases": biases.T,
        "wo": np.asarray(L0_rec_Wo).reshape(2, P).T,
        "bo": np.asarray(L0_rec_bo).reshape(1, 1),
    }
    given = {k: np.ascontiguousarray(v) for k, v in given.items()}
    nc = bacc.Bacc("TRN2", target_bir_lowering=False, num_devices=1)
    ap = {k: nc.dram_tensor(k, v.shape, mybir.dt.from_np(v.dtype), kind="ExternalInput").ap()
          for k, v in given.items()}
    out = nc.dram_tensor("out", (B, 1), F32, kind="ExternalOutput").ap()
    dlrm(nc, ap["xT"], ap["idx"], ap["table"], ap["ident"], ap["w1"],
         {k: ap["w_" + k] for k in LAYERS}, ap["biases"], ap["wo"], ap["bo"], out)
    r = run_bass_kernel_spmd(nc, [given], core_ids=[0])
    return r.results[0]["out"]
```

```python
import numpy as np
import concourse.bass as bass
from concourse import mybir
from contextlib import ExitStack

F32 = mybir.dt.float32
F32R = mybir.dt.float32r
I32 = mybir.dt.int32
U32 = mybir.dt.uint32
ALU = mybir.AluOpType
ACT = mybir.ActivationFunctionType

P = 128
B, CONT, CATS, VOCAB, E = 2048, 13, 26, 12500, 128
FEATS = CATS + 1
PAIRS = FEATS * CATS // 2
CHUNK = 512
CHUNKS = B // CHUNK
HALF = CHUNK // 2
PARTS = [(0, HALF), (HALF, HALF)] + [(c * CHUNK, CHUNK) for c in range(1, CHUNKS)]
TILES = B // P
S = 4
GROUPS = P // S
UNIT = 16
UNITS = GROUPS // UNIT
J = 32
BANKS = 4

FIRST_PAIR = [sum(FEATS - 1 - r for r in range(i)) for i in range(CATS)]
PAIR_BLOCKS = [(r, min(P, PAIRS - r)) for r in range(0, PAIRS, P)]
X_BLOCKS = PAIR_BLOCKS + [(PAIRS, E)]
FLIPS = [list(range(c, min(c + 4, CATS))) for c in range(0, CATS, 4)]
REGROUPS = [list(range(a, b)) for a, b in zip([0, 4, 8, 11, 14, 17, 20, 23], [4, 8, 11, 14, 17, 20, 23, 26])]

FULL = lambda n: [(k, P) for k in range(n)]
LAYERS = {
    "d2": ("h1", "h2", FULL(4), 2, 4),
    "df": ("h2", "dense", FULL(2), 1, 6),
    "t1": ("x", "h1", [(3, P)] + [(k, n) for k, (_, n) in enumerate(PAIR_BLOCKS)], 8, 7),
    "t2": ("h1", "h2", FULL(8), 8, 15),
    "t3": ("h2", "h1", FULL(8), 4, 23),
    "t4": ("h1", "h4", FULL(4), 2, 27),
}
BIASES = 29
TOGETHER = {"d2": 2, "df": 1, "t1": 2, "t2": 1, "t3": 1, "t4": 1}

def bottom(chunk):
    both = [(c * CHUNK, CHUNK) for c in (chunk, chunk + 1)]
    out = [("spread", part, m) for part in both for m in range(4)]
    for layer in ("d2", "df"):
        out += strips_of(both[0], layer) + [("again", *s[1:]) for s in strips_of(both[1], layer)]
    return out


def strips_of(part, *layers):
    return [("again" if m % TOGETHER[layer] else "strip", part, layer, m)
            for layer in layers for m in range(LAYERS[layer][3])]


def rest(part):
    return strips_of(part, "t2", "t3", "t4")


def features(part, k):
    return [("flip", part, k, 0), ("flip", part, k, 1), ("pair", part, k)]


def stacks(part):
    return [("dense", part)] + [("stack", part, b) for b in range(len(PAIR_BLOCKS))]


def mixed(part, following, features_at):
    strips = rest(part)
    before = {n: [] for n in range(len(strips))}
    for k, n in enumerate(features_at):
        for more, s in enumerate(features(following, k)):
            before[n + more].append(s)
    out = []
    for n, s in enumerate(strips):
        out += before[n] + [s]
    out += [("regroup", following, 0), ("out", part), ("regroup", following, 1)]
    return out + stacks(following) + strips_of(following, "t1")


def half(part, between):
    out = [("regroup", part, 0), ("regroup", part, 1)] + stacks(part)
    for m, s in enumerate(strips_of(part, "t1")):
        out += [between[m], s] if m in between else [s]
    return out


HALVES = {"flip": (range(0, 4), range(4, len(FLIPS))), "regroup": (range(0, 4), range(4, len(REGROUPS)))}


def counts(step):
    kind = step[0]
    split = kind in ("spread", "stack") or (kind in ("strip", "again") and step[2] not in ("df", "t4"))
    return {"acc": int(kind in ("spread", "strip", "again", "stack", "out")), "split": int(split),
            "strip": int(kind == "strip"),
            "bank": len(HALVES[kind][step[-1]]) if kind in HALVES else 0,
            "unit": UNITS if kind == "pair" else 0, "tile": int(kind == "flip" and step[-1] == 1),
            "dense": int(kind == "dense")}


KINDS = ("acc", "split", "strip", "bank", "unit", "tile", "dense")


def total(steps):
    return {k: sum(counts(s)[k] for s in steps) for k in KINDS}


def plus(*many):
    return {k: sum(m[k] for m in many) for k in KINDS}


class Place:

    def __init__(self, local, base, each, it):
        self.local, self.base, self.each, self.it = local, base, each, it

    def at(self, kind, more=0):
        return self.it * self.each[kind] + (self.base[kind] + self.local[kind] + more)

    def slot(self, kind, more=0):
        return (self.base[kind] + self.local[kind] + more) % 2


def walk(steps, base, it):
    local = {k: 0 for k in KINDS}
    each = total(steps)
    for step in steps:
        yield step, Place(dict(local), base, each, it)
        local = plus(local, counts(step))


FEATURES_AT = (0, 4, 8, 11)
THIRD_AT = (2, 3, 4)
FIRST_HALF, SECOND_HALF = PARTS[:2]
FIRST, SECOND, LAST = (0, CHUNK), PARTS[2], PARTS[-1]


START = (bottom(0) + features(FIRST_HALF, 0) + bottom(2) + features(FIRST_HALF, 1)
         + half(FIRST_HALF, dict(zip(THIRD_AT, features(SECOND_HALF, 0))))
         + features(SECOND_HALF, 1) + half(SECOND_HALF, {}))
BODY = mixed(FIRST, SECOND, FEATURES_AT)
END = rest(LAST) + [("out", LAST)]


def strips_ahead(steps, n):
    later = [s[0] for s in steps[n + 1:] if s[0] in ("strip", "again")]
    if steps[n][0] not in ("strip", "again") or later[:1] == ["again"]:
        return 0
    return 2 if steps[n][0] == "strip" else 1


def blocks_of(steps, number):
    strips = [s for s in steps if s[0] == "strip"]
    layer = strips[number][2] if number < len(strips) else "t2"
    return len(LAYERS[layer][2]) * TOGETHER[layer]


def splits_since(steps, n, k):
    _, part, layer, _ = steps[n]
    since = 0
    for s in reversed(steps[:n]):
        since += counts(s)["split"]
        made = None
        if s[0] == "spread":
            made = ("h1", s[2])
        elif s[0] in ("strip", "again"):
            made = (LAYERS[s[2]][1], s[3])
        if s[1] == part and made == (LAYERS[layer][0], k):
            return since
    return since + LAYERS["t1"][3] - k


ZERO = {k: 0 for k in KINDS}
AFTER_START = total(START)
AFTER_BODY = plus(AFTER_START, *[total(BODY)] * (CHUNKS - 1))


def dlrm(nc, xT, idx, table, ident, w1, w, biases, wo, bo, out):
    ctx = ExitStack()
    with ctx:
        def sb(name, shape, dt=F32):
            return ctx.enter_context(nc.sbuf_tensor(name, shape, dt))

        def sem(name):
            return ctx.enter_context(nc.semaphore(name))

        gathered = sb("gathered", [P, 2, CATS, E])
        feats = sb("feats", [P, GROUPS, S, FEATS])
        prods = sb("prods", [P, CHUNK // S, CATS])
        rows = sb("rows", [P, S, PAIRS])
        wide_x = sb("wide_x", [P, B], F32R)
        wide_w = sb("wide_w", [P, 512], F32R)
        x = sb("x", [P, 2, len(X_BLOCKS), CHUNK], F32R)
        h1 = sb("h1", [P, 2, 8, CHUNK], F32R)
        h2 = sb("h2", [P, 2, 8, CHUNK], F32R)
        h4 = sb("h4", [P, 2, CHUNK])
        whole = sb("whole", [P, 2, CHUNK])
        dense = sb("dense", [P, B])
        raw = sb("raw", [P, 2, 8, P])
        strip = sb("strip", [P, 2, 2, 8, P], F32R)
        eye = sb("eye", [P, P])
        bias = sb("bias", [P, BIASES])
        wo_s = sb("wo_s", [P, 2])
        bo_s = sb("bo_s", [1, 1])
        cat = sb("cat", [P, TILES, CATS], I32)
        first_row = sb("first_row", [P, TILES, CATS], I32)
        row_of = sb("row_of", [P, TILES, CATS], U32)
        tile_rows = sb("tile_rows", [P, 2, CATS], U32)
        y = sb("y", [1, B])

        bank = ctx.enter_context(nc.psum_tensor("bank", [P, BANKS, 512], F32))
        unit = ctx.enter_context(nc.psum_tensor("unit", [P, 2, 512], F32))
        acc = ctx.enter_context(nc.psum_tensor("acc", [P, 2, CHUNK], F32))

        wide_in = sem("wide_in")
        constants_in = sem("constants_in")
        cat_in = sem("cat_in")
        raw_in = [sem("raw_in0"), sem("raw_in1")]
        gather_in = [sem("gather_in0"), sem("gather_in1")]
        y_out = sem("y_out")
        zeroed = sem("zeroed")
        first_row_set = sem("first_row_set")
        cat_step = sem("cat_step")
        rows_set = sem("rows_set")
        rows_seen = sem("rows_seen")
        unit_zeroed = sem("unit_zeroed")
        wide_h = sem("wide_h")
        wide_ready = sem("wide_ready")
        low_w = sem("low_w")
        low_y = sem("low_y")
        low_dense = sem("low_dense")
        even_bank_read = sem("even_bank_read")
        even_unit_read = sem("even_unit_read")
        tile_flipped = sem("tile_flipped")
        high_w = sem("high_w")
        acc_read = sem("acc_read")
        high_dense = sem("high_dense")
        odd_bank_read = sem("odd_bank_read")
        odd_unit_read = sem("odd_unit_read")
        acc_done = sem("acc_done")
        bank_done = sem("bank_done")
        unit_done = sem("unit_done")

        regions = {"x": x, "h1": h1, "h2": h2}
        feats_flat = feats[:].rearrange("p g s j -> p (g s j)")
        wide_x_raw, wide_w_raw = feats_flat[:, 0:B], feats_flat[:, B:B + 512]
        products = [unit[:, u, 0:UNIT * CATS].rearrange("p (g i) -> p g i", i=CATS) for u in range(2)]
        wrapped = prods[:, 0:TILES, :]
        block = ctx.enter_context(nc.Block())

        def columns(step, p):
            return bass.ds(p.it * CHUNK + step[1][0], step[1][1])

        def inside(step):
            first, width = step[1]
            return slice(first % CHUNK, first % CHUNK + width)

        def place(step, region, k):
            second = (step[0] == "spread" or step[2] in ("d2", "df")) and step[1][0] // CHUNK % 2
            return k + second * {"h1": 4, "h2": 2}.get(region, 0)

        def acc_target(step, p):
            if step[0] == "spread":
                return P, [h1[:, a, place(step, "h1", step[2]), :] for a in range(2)], None, step[2]
            if step[0] == "stack":
                n = PAIR_BLOCKS[step[2]][1]
                return n, [x[0:n, a, step[2], inside(step)] for a in range(2)], None, None
            _, dst, _, _, first = LAYERS[step[2]]
            m = step[3]
            if dst == "dense":
                return P, None, dense[:, columns(step, p)], first
            if dst == "h4":
                return P, None, h4[:, m, inside(step)], first + m
            return P, [regions[dst][:, a, place(step, dst, m), inside(step)] for a in range(2)], None, first + m

        def dense_written(eng, step):
            eng.wait_ge(acc_read, 2 + (total(bottom(0)) if step[1] in PARTS[:2] else AFTER_START)["acc"])

        def bank_copies(kind, part, n, slot):
            if kind == "flip":
                c, m = FLIPS[n][0], len(FLIPS[n])
                return [(feats[:, :, :, c:c + m].rearrange("p g s c -> p c s g"),
                         bank[:, slot, 0:m * P].rearrange("p (c s g) -> p c s g", c=m, s=S))]
            groups = part[1] // S
            return [(rows[0:groups, :, FIRST_PAIR[i]:FIRST_PAIR[i] + CATS - i],
                     bank[0:groups, slot, q * P:(q + 1) * P].rearrange("p (s j) -> p s j", s=S)[:, :, i + 1:FEATS])
                    for q, i in enumerate(REGROUPS[n])]

        def unit_target(k, u):
            return prods[:, k * GROUPS + u * UNIT:k * GROUPS + (u + 1) * UNIT, :]

        @block.sync
        def _(sp):
            sp.dma_start(cat[:], idx).then_inc(cat_in, 16)
            sp.wait_ge(zeroed, 1)
            for q in range(4):
                sp.dma_start(wide_w_raw[32 * q:32 * q + CONT], w1).then_inc(wide_in, 16)
                sp.dma_start(wide_x_raw[32 * q:32 * q + CONT], xT).then_inc(wide_in, 16)

            def load_strip(step, p):
                layer, m = step[2], step[3]
                slot = p.slot("strip")
                sp.wait_ge(low_w, p.at("strip", 1))
                cols = slice(m * P, (m + TOGETHER[layer]) * P)
                to = raw[:, slot].rearrange("p (k o) n -> p k (o n)", o=TOGETHER[layer])
                if layer == "t1":
                    a, c = PAIR_BLOCKS[2]
                    sp.dma_start(to[:, 0:2], w[layer][0:a, cols].rearrange("(k p) n -> p k n", p=P)
                                 ).then_inc(raw_in[slot], 16)
                    sp.dma_start(to[0:c, 2], w[layer][a:a + c, cols]).then_inc(raw_in[slot], 16)
                    sp.dma_start(to[:, 3], w[layer][PAIRS:PAIRS + E, cols]).then_inc(raw_in[slot], 16)
                else:
                    n = len(LAYERS[layer][2])
                    for k0, k1 in ((0, n // 2), (n // 2, n)):
                        sp.dma_start(to[:, k0:k1], w[layer][k0 * P:k1 * P, cols].rearrange("(k p) n -> p k n", p=P)
                                     ).then_inc(raw_in[slot], 16)
                    sp.sem_inc(raw_in[slot], 16)

            def phase(steps, base, it):
                for step, p in walk(steps, base, it):
                    if step[0] == "strip":
                        load_strip(step, p)

            phase(START, ZERO, 0)
            with sp.Fori(0, CHUNKS - 1) as i:
                phase(BODY, AFTER_START, i)
            phase(END, AFTER_BODY, 0)
            sp.wait_ge(acc_read, 2 + AFTER_BODY["acc"] + total(END)["acc"])
            sp.dma_start(out.rearrange("b o -> o b"), y[:]).then_inc(y_out, 16)
            sp.wait_ge(y_out, 16)

        @block.gpsimd
        def _(pool):
            nc.gpsimd.iota(first_row[:], pattern=[[0, TILES], [VOCAB, CATS]], base=0,
                           channel_multiplier=0).then_inc(first_row_set, 1)
            def gather(t, k, copies):
                nc.gpsimd.tensor_copy(tile_rows[:, k, :], row_of[:, t, :]).then_inc(rows_set, 1)
                pool.wait_ge(rows_set, copies)
                pool.sem_inc(rows_seen, 1)
                for c in range(CATS):
                    nc.gpsimd.indirect_dma_start(
                        gathered[:, k, c, :], None, table,
                        bass.IndirectOffsetOnAxis(tile_rows[:, k, c:c + 1], 0)).then_inc(gather_in[k], 16)

            for k in range(2):
                pool.wait_ge(cat_step, 4 * (k + 1))
                gather(k, k, k + 1)
            with pool.Fori(1, TILES // 2) as i:
                for k in range(2):
                    pool.wait_ge(tile_flipped, i * 2 + k - 1)
                    gather(i * 2 + k, k, i * 2 + k + 1)

        @block.vector
        def _(dve):
            nc.vector.memset(feats_flat[:, 0:B + 512], 0.0).then_inc(zeroed, 1)
            dve.wait_ge(cat_in, 16)
            dve.wait_ge(first_row_set, 1)
            for n, tiles in enumerate((slice(0, 1), slice(1, TILES))):
                given, kept = cat[:, tiles], wrapped[:, tiles]
                nc.vector.tensor_scalar(kept, given, 0.0, float(VOCAB), ALU.is_lt, ALU.mult).then_inc(cat_step, 1)
                dve.wait_ge(cat_step, 4 * n + 1)
                nc.vector.tensor_tensor(kept, given, kept, ALU.add).then_inc(cat_step, 1)
                dve.wait_ge(cat_step, 4 * n + 2)
                nc.vector.tensor_scalar(kept, kept, 0.0, float(VOCAB - 1), ALU.max, ALU.min).then_inc(cat_step, 1)
                dve.wait_ge(cat_step, 4 * n + 3)
                nc.vector.tensor_tensor(row_of[:, tiles], kept, first_row[:, tiles], ALU.add).then_inc(cat_step, 1)
            for k in range(2):
                nc.vector.memset(raw[:, k], 0.0).then_inc(low_w, 1)
            dve.sem_inc(low_y, 1)
            dve.wait_ge(wide_in, 16 * 8)
            nc.vector.tensor_copy(wide_w[:], wide_w_raw).then_inc(wide_h, 1)
            nc.vector.tensor_copy(wide_x[:, 0:CHUNK], wide_x_raw[:, 0:CHUNK]).then_inc(wide_h, 1)
            nc.vector.tensor_copy(wide_x[:, CHUNK:B], wide_x_raw[:, CHUNK:B]).then_inc(wide_h, 1)
            dve.wait_ge(wide_h, 1)
            for q in (32, 96):
                nc.vector.tensor_tensor(wide_w[q:q + 32], wide_w_raw[q:q + 32], wide_w[q:q + 32].bitcast(F32),
                                        ALU.subtract)
            for n, cols in enumerate((slice(0, CHUNK), slice(CHUNK, B))):
                dve.wait_ge(wide_h, n + 2)
                nc.vector.tensor_tensor(wide_x[64:128, cols], wide_x_raw[64:128, cols],
                                        wide_x[64:128, cols].bitcast(F32), ALU.subtract).then_inc(wide_ready, 1)
            nc.vector.memset(unit[:], 0.0).then_inc(unit_zeroed, 1)

            def split_strip(p, more, blocks):
                slot = p.slot("strip", more)
                dve.wait_ge(high_w, p.at("strip", more + 1))
                nc.vector.tensor_tensor(strip[:, slot, 1, 0:blocks, :], raw[:, slot, 0:blocks, :],
                                        strip[:, slot, 0, 0:blocks, :].bitcast(F32), ALU.subtract
                                        ).then_inc(low_w, 1)

            def phase(steps, base, it, last=False):
                strips = [s for s in steps if s[0] == "strip"]
                for at_step, (step, p) in enumerate(walk(steps, base, it)):
                    kind = step[0]
                    more = strips_ahead(steps, at_step)
                    if more and not (last and p.local["strip"] + more >= len(strips)):
                        split_strip(p, more, blocks_of(steps, p.local["strip"] + more))
                    if counts(step)["split"]:
                        height, parts, _, _ = acc_target(step, p)
                        dve.wait_ge(acc_read, p.at("acc", 3))
                        read = (acc if kind == "stack" else whole)[0:height, p.slot("acc"), 0:step[1][1]]
                        nc.vector.tensor_tensor(parts[1], read, parts[0].bitcast(F32), ALU.subtract
                                                ).then_inc(low_y, 1)
                    if kind in HALVES:
                        for g, n in enumerate(HALVES[kind][step[-1]]):
                            number = p.base["bank"] + p.local["bank"] + g
                            if number % 2 == 0:
                                dve.wait_ge(bank_done, p.at("bank", g + 1))
                                for to, source in bank_copies(kind, step[1], n, number % BANKS):
                                    last_read = nc.vector.tensor_copy(to, source)
                                last_read.then_inc(even_bank_read, 1)
                    if kind == "flip" and step[-1] == 1:
                        dve.wait_ge(bank_done, p.at("bank", counts(step)["bank"]))
                        dense_written(dve, step)
                        nc.vector.tensor_copy(
                            feats[:, :, :, CATS].rearrange("p g s -> p s g"),
                            dense[:, columns(step, p)].rearrange("p (s t g) -> p t s g", s=S, g=GROUPS)[:, step[2]]
                        ).then_inc(tile_flipped, 1)
                    if kind == "pair":
                        for u in range(0, UNITS, 2):
                            dve.wait_ge(unit_done, p.at("unit", u + 1))
                            nc.vector.tensor_copy(unit_target(step[2], u), products[0]).then_inc(even_unit_read, 1)
                    if kind == "dense":
                        dve.wait_ge(high_dense, p.at("dense", 1))
                        nc.vector.tensor_tensor(x[:, 1, 3, inside(step)], dense[:, columns(step, p)],
                                                x[:, 0, 3, inside(step)].bitcast(F32), ALU.subtract).then_inc(low_dense, 1)

            for more in range(2):
                split_strip(Place(ZERO, ZERO, ZERO, 0), more, blocks_of(START, more))
            phase(START, ZERO, 0)
            with dve.Fori(0, CHUNKS - 1) as i:
                phase(BODY, AFTER_START, i)
            phase(END, AFTER_BODY, 0, last=True)

        @block.scalar
        def _(act):
            act.sem_inc(acc_read, 2)
            for to, given in ((bias, biases), (eye, ident), (wo_s, wo), (bo_s, bo)):
                act.dma_start(to[:], given).then_inc(constants_in, 16)
            act.wait_ge(constants_in, 16 * 4)

            def split_strip(p, more, blocks):
                slot = p.slot("strip", more)
                n = p.base["strip"] + p.local["strip"] + more
                act.wait_ge(raw_in[slot], p.it * (24 * p.each["strip"]) + 48 * (n // 2 + 1))
                nc.scalar.activation(strip[:, slot, 0, 0:blocks, :], raw[:, slot, 0:blocks, :],
                                     ACT.Copy).then_inc(high_w, 1)

            def splits_before(steps, p, n):
                return sum(counts(s)["split"] for s, q in walk(steps, ZERO, 0) if counts(s)["acc"] and q.local["acc"] <= n)

            def phase(steps, base, it, last=False):
                strips = [s for s in steps if s[0] == "strip"]
                for at_step, (step, p) in enumerate(walk(steps, base, it)):
                    kind = step[0]
                    if counts(step)["acc"]:
                        act.wait_ge(acc_done, p.at("acc", 1))
                    more = strips_ahead(steps, at_step)
                    if more and not (last and p.local["strip"] + more >= len(strips)):
                        split_strip(p, more, blocks_of(steps, p.local["strip"] + more))
                    if kind in ("spread", "strip", "again", "stack"):
                        height, parts, plain, column = acc_target(step, p)
                        slot = p.slot("acc")
                        width = step[1][1]
                        source = acc[0:height, slot, 0:width]
                        func, b = (ACT.Copy, 0.0) if column is None else (ACT.Relu, bias[:, column:column + 1])
                        if parts is None:
                            nc.scalar.activation(plain, source, func, bias=b).then_inc(acc_read, 1)
                        elif kind == "stack":
                            nc.scalar.activation(parts[0], source, func, bias=b).then_inc(acc_read, 1)
                        else:
                            before = splits_before(steps, p, p.local["acc"] - 2)
                            act.wait_ge(low_y, p.it * p.each["split"] + (1 + p.base["split"] + before))
                            nc.scalar.activation(whole[0:height, slot, 0:width], source, func, bias=b)
                            nc.scalar.activation(parts[0], source, func, bias=b).then_inc(acc_read, 1)
                    if kind == "out":
                        nc.scalar.activation(y[0:1, columns(step, p)], acc[0:1, p.slot("acc"), 0:step[1][1]],
                                             ACT.Sigmoid, bias=bo_s[0:1, 0:1]).then_inc(acc_read, 1)
                    if kind in HALVES:
                        for g, n in enumerate(HALVES[kind][step[-1]]):
                            number = p.base["bank"] + p.local["bank"] + g
                            if number % 2 == 1:
                                act.wait_ge(bank_done, p.at("bank", g + 1))
                                for to, source in bank_copies(kind, step[1], n, number % BANKS):
                                    last_read = nc.scalar.activation(to, source, ACT.Copy)
                                last_read.then_inc(odd_bank_read, 1)
                    if kind == "pair":
                        for u in range(1, UNITS, 2):
                            act.wait_ge(unit_done, p.at("unit", u + 1))
                            nc.scalar.activation(unit_target(step[2], u), products[1], ACT.Copy
                                                 ).then_inc(odd_unit_read, 1)
                    if kind == "dense":
                        dense_written(act, step)
                        nc.scalar.activation(x[:, 0, 3, inside(step)], dense[:, columns(step, p)],
                                             ACT.Copy).then_inc(high_dense, 1)

            for more in range(2):
                split_strip(Place(ZERO, ZERO, ZERO, 0), more, blocks_of(START, more))
            phase(START, ZERO, 0)
            with act.Fori(0, CHUNKS - 1) as i:
                phase(BODY, AFTER_START, i)
            phase(END, AFTER_BODY, 0, last=True)

        @block.tensor
        def _(pe):
            pe.wait_ge(constants_in, 16 * 4)

            def half_at(p, kind, more, even=False):
                return p.it * (p.each[kind] // 2) + (p.base[kind] + p.local[kind] + more + even) // 2

            def phase(steps, base, it):
                after_h4 = 0
                for at_step, (step, p) in enumerate(walk(steps, base, it)):
                    kind = step[0]
                    after_h4 = 0 if kind in ("strip", "again") else after_h4 + counts(step)["acc"]
                    slot = p.slot("acc")
                    width = step[1][1]
                    if counts(step)["acc"]:
                        pe.wait_ge(acc_read, p.at("acc", 1))
                        used = [s for s in steps[:at_step] if counts(s)["acc"]][-2:]
                        if len(used) == 2 and used[0][0] == "stack":
                            pe.wait_ge(low_y, p.at("split", 1 - counts(used[1])["split"]))
                    if kind == "spread":
                        m = step[2]
                        pe.wait_ge(wide_ready, 1 if step[1][0] == 0 else 2)
                        nc.tensor.matmul(acc[:, slot, :], wide_w[:, m * P:(m + 1) * P],
                                         wide_x[:, columns(step, p)],
                                         start=True, stop=True).then_inc(acc_done, 1)
                    if kind in ("strip", "again"):
                        src, _, blocks, _, _ = LAYERS[step[2]]
                        m = step[3]
                        region = regions[src]
                        together = TOGETHER[step[2]]
                        again = int(kind == "again")
                        w_slot = p.slot("strip", -again)
                        pe.wait_ge(low_w, p.at("strip", 3 - again))
                        if m == 0 and src == "x":
                            pe.wait_ge(low_dense, p.at("dense"))
                        for n, (k, height) in enumerate(blocks):
                            if m == 0 and src != "x":
                                pe.wait_ge(low_y, p.at("split", 2 - splits_since(steps, at_step, k)))
                            if m == 0 and src == "x" and n > 0:
                                pe.wait_ge(low_y, p.at("split", 2 + k - len(PAIR_BLOCKS)))
                            for a, b in ((0, 0), (0, 1), (1, 0)):
                                last_mm = nc.tensor.matmul(
                                    acc[:, slot, 0:width], strip[0:height, w_slot, a, k * together + m % together, :],
                                    region[0:height, b, place(step, src, k), inside(step)],
                                    start=(n == 0 and (a, b) == (0, 0)),
                                    stop=(n == len(blocks) - 1 and (a, b) == (1, 0)))
                        last_mm.then_inc(acc_done, 1)
                    if kind == "out":
                        pe.wait_ge(acc_read, p.at("acc", 2 - (after_h4 - 1)))
                        for k in range(2):
                            last_mm = nc.tensor.matmul(acc[0:1, slot, 0:width], wo_s[:, k:k + 1], h4[:, k, 0:width],
                                                       start=(k == 0), stop=(k == 1))
                        last_mm.then_inc(acc_done, 1)
                    if kind in HALVES:
                        if kind == "flip":
                            number = p.base["tile"] + p.local["tile"]
                            pe.wait_ge(gather_in[number % 2], p.it * (8 * CATS * p.each["tile"]) + 16 * CATS * (number // 2 + 1))
                        else:
                            pe.wait_ge(even_unit_read, half_at(p, "unit", 0))
                            pe.wait_ge(odd_unit_read, half_at(p, "unit", 0))
                        for g, n in enumerate(HALVES[kind][step[-1]]):
                            number = p.base["bank"] + p.local["bank"] + g
                            if number >= BANKS:
                                pe.wait_ge((even_bank_read, odd_bank_read)[number % 2], half_at(p, "bank", g - 2))
                            for q, one in enumerate((FLIPS, REGROUPS)[kind == "regroup"][n]):
                                source = gathered[:, step[2] % 2, one, :] if kind == "flip" else prods[:, 0:width // S, one]
                                height = P if kind == "flip" else width // S
                                last_t = nc.tensor.transpose(bank[0:height, number % BANKS, q * P:(q + 1) * P],
                                                             source, eye[:])
                            last_t.then_inc(bank_done, 1)
                    if kind == "pair":
                        pe.wait_ge(tile_flipped, p.at("tile"))
                        pe.wait_ge(odd_bank_read, half_at(p, "bank", 0))
                        for u in range(UNITS):
                            number = p.base["unit"] + p.local["unit"] + u
                            if number == 0:
                                pe.wait_ge(unit_zeroed, 1)
                            if number >= 2:
                                pe.wait_ge((even_unit_read, odd_unit_read)[number % 2], half_at(p, "unit", u))
                            for v in range(UNIT):
                                for s in range(S):
                                    one = feats[:, u * UNIT + v, s, :]
                                    last_mm = nc.tensor.matmul(
                                        unit[J * s:J * s + FEATS, number % 2, v * CATS:(v + 1) * CATS],
                                        one, one[:, 0:CATS], start=True, stop=True)
                            last_mm.then_inc(unit_done, 1)
                    if kind == "stack":
                        first, n = PAIR_BLOCKS[step[2]]
                        if step[2] == 0:
                            for read in (even_bank_read, odd_bank_read):
                                pe.wait_ge(read, half_at(p, "bank", 0, even=read is even_bank_read))
                        for s in range(S):
                            groups = width // S
                            last_t = nc.tensor.transpose(acc[0:n, slot, s * groups:(s + 1) * groups],
                                                         rows[0:groups, s, first:first + n],
                                                         eye[0:groups, 0:groups])
                        last_t.then_inc(acc_done, 1)

            phase(START, ZERO, 0)
            with pe.Fori(0, CHUNKS - 1) as i:
                phase(BODY, AFTER_START, i)
            phase(END, AFTER_BODY, 0)


def kernel(r_dense_x, r_cat_idx, L0_rec_emb_table, L0_rec_Wd1, L0_rec_bd1, L0_rec_Wd2, L0_rec_bd2,
           L0_rec_Wdf, L0_rec_bdf, L0_rec_Wt1, L0_rec_bt1, L0_rec_Wt2, L0_rec_bt2, L0_rec_Wt3,
           L0_rec_bt3, L0_rec_Wt4, L0_rec_bt4, L0_rec_Wo, L0_rec_bo):
    import concourse.bacc as bacc
    from concourse.bass_utils import run_bass_kernel_spmd

    idx = np.asarray(r_cat_idx)
    idx = np.concatenate([idx[a:a + n].reshape(S, n // P, GROUPS, CATS).transpose(0, 2, 1, 3) for a, n in PARTS], axis=2)
    biases = np.concatenate([np.asarray(b).reshape(-1, P) for b in (
        L0_rec_bd1, L0_rec_bd2, L0_rec_bdf, L0_rec_bt1, L0_rec_bt2, L0_rec_bt3, L0_rec_bt4)])
    given = {
        "xT": np.asarray(r_dense_x).T,
        "idx": idx.reshape(P, TILES, CATS),
        "table": np.asarray(L0_rec_emb_table).reshape(CATS * VOCAB, E),
        "ident": np.eye(P, dtype=np.float32),
        "w1": L0_rec_Wd1,
        "w_d2": L0_rec_Wd2, "w_df": L0_rec_Wdf,
        "w_t1": L0_rec_Wt1, "w_t2": L0_rec_Wt2, "w_t3": L0_rec_Wt3, "w_t4": L0_rec_Wt4,
        "biases": biases.T,
        "wo": np.asarray(L0_rec_Wo).reshape(2, P).T,
        "bo": np.asarray(L0_rec_bo).reshape(1, 1),
    }
    given = {k: np.ascontiguousarray(v) for k, v in given.items()}
    nc = bacc.Bacc("TRN2", target_bir_lowering=False, num_devices=1)
    ap = {k: nc.dram_tensor(k, v.shape, mybir.dt.from_np(v.dtype), kind="ExternalInput").ap()
          for k, v in given.items()}
    out = nc.dram_tensor("out", (B, 1), F32, kind="ExternalOutput").ap()
    dlrm(nc, ap["xT"], ap["idx"], ap["table"], ap["ident"], ap["w1"],
         {k: ap["w_" + k] for k in LAYERS}, ap["biases"], ap["wo"], ap["bo"], out)
    r = run_bass_kernel_spmd(nc, [given], core_ids=[0])
    return r.results[0]["out"]
```
